# Optimizing a Trainium2 kernel written in Bass

```python
import numpy as np
import jax
import jax.numpy as jnp

def _softmax(x, axis=-1):
    return jax.nn.softmax(x, axis=axis)

def _gelu(x):
    return jax.nn.gelu(x, approximate=True)

def _silu(x):
    return jax.nn.silu(x)

def _sigmoid(x):
    return jax.nn.sigmoid(x)

def _layernorm(x, axis=-1, eps=1e-05):
    m = jnp.mean(x, axis=axis, keepdims=True)
    v = jnp.var(x, axis=axis, keepdims=True)
    return (x - m) / jnp.sqrt(v + eps)

def _scatter_add(tgt, idx, src, axis=0):
    return tgt.at[idx].add(src)

def _segment_sum(src, seg, n):
    return jax.ops.segment_sum(src, seg, n)
kernel_name = 'mk_macaron_d1_jaxref_r8_4761d8'

def setup_inputs(seed: int=0):
    np.random.seed(seed)
    _w = jnp.asarray

    def _L0_attn_setup():
        import jax, jax.numpy as jnp
        import numpy as np
        B, S, D = (2, 256, 256)
        H = 16
        HD = D // H
        key = jax.random.key(seed)
        ks = jax.random.split(key, 6)
        s = 1.0 / np.sqrt(D)
        return {'inputs': jax.random.normal(ks[0], (B, S, D), dtype=jnp.float32), 'w_q': jax.random.normal(ks[1], (D, D), dtype=jnp.float32) * s, 'w_k': jax.random.normal(ks[2], (D, D), dtype=jnp.float32) * s, 'w_v': jax.random.normal(ks[3], (D, D), dtype=jnp.float32) * s, 'w_o': jax.random.normal(ks[4], (D, D), dtype=jnp.float32) * s, 'b_o': jax.random.normal(ks[5], (D,), dtype=jnp.float32) * 0.02}
    _L0_attn_in = _L0_attn_setup()

    def _L0_ffn_setup():
        import jax, jax.numpy as jnp
        import numpy as np
        NUM_EXPERTS = 8
        TOP_K = 2
        key = jax.random.key(seed)
        ks = jax.random.split(key, 5)
        B, L, D, H = (2, 256, 256, 512)
        return {'layer_input': jax.random.normal(ks[0], (B, L, D), jnp.float32), 'router_weight': jax.random.normal(ks[1], (NUM_EXPERTS, D), jnp.float32) * 0.02, 'w_in': jax.random.normal(ks[2], (NUM_EXPERTS, 2 * H, D), jnp.float32) * 0.02, 'w_out': jax.random.normal(ks[3], (NUM_EXPERTS, D, H), jnp.float32) * 0.02, 'bias': jax.random.normal(ks[4], (D,), jnp.float32) * 0.02}
    _L0_ffn_in = _L0_ffn_setup()
    _d = {'L0_attn_inputs': _L0_attn_in['inputs'], 'L0_attn_w_q': _L0_attn_in['w_q'], 'L0_attn_w_k': _L0_attn_in['w_k'], 'L0_attn_w_v': _L0_attn_in['w_v'], 'L0_attn_w_o': _L0_attn_in['w_o'], 'L0_attn_b_o': _L0_attn_in['b_o'], 'L0_ffn_router_weight': _L0_ffn_in['router_weight'], 'L0_ffn_w_in': _L0_ffn_in['w_in'], 'L0_ffn_w_out': _L0_ffn_in['w_out'], 'L0_ffn_bias': _L0_ffn_in['bias']}
    _x0 = _d['L0_attn_inputs']
    _d['L0_attn_inputs'] = jax.random.normal(jax.random.fold_in(jax.random.key(seed), 1), (4, 256, 256), dtype=_x0.dtype)
    del _x0
    return _d

def reference(L0_attn_inputs, L0_attn_w_q, L0_attn_w_k, L0_attn_w_v, L0_attn_w_o, L0_attn_b_o, L0_ffn_router_weight, L0_ffn_w_in, L0_ffn_w_out, L0_ffn_bias):

    def _L0_attn_ref(inputs, w_q, w_k, w_v, w_o, b_o):
        import jax, jax.numpy as jnp
        import numpy as np
        B, S, D = (2, 256, 256)
        H = 16
        HD = D // H
        b, t, _ = inputs.shape
        q = (inputs @ w_q.T).reshape(b, t, H, HD)
        k = (inputs @ w_k.T).reshape(b, t, H, HD)
        v = (inputs @ w_v.T).reshape(b, t, H, HD)
        scores = jnp.einsum('bqhd,bkhd->bhqk', q, k)
        causal = jnp.triu(jnp.ones((t, t), dtype=bool), k=1)
        scores = jnp.where(causal, -jnp.inf, scores)
        scale = jnp.float32(t) ** 0.5
        attn = jax.nn.softmax(scores / scale, axis=-1)
        ctx = jnp.einsum('bhqk,bkhd->bqhd', attn, v).reshape(b, t, D)
        return ctx @ w_o.T + b_o

    def _L0_ffn_ref(layer_input, router_weight, w_in, w_out, bias):
        import jax, jax.numpy as jnp
        import numpy as np
        NUM_EXPERTS = 8
        TOP_K = 2
        B, L, D = layer_input.shape
        x = layer_input.reshape(-1, D)
        T = x.shape[0]
        logits = (x @ router_weight.T).astype(jnp.float32)
        top_vals, top_idx = jax.lax.top_k(logits, TOP_K)
        top_gates = jax.nn.softmax(top_vals, axis=1).astype(x.dtype)
        dense_gates = jnp.zeros((T, NUM_EXPERTS), x.dtype)
        dense_gates = dense_gates.at[jnp.arange(T)[:, None], top_idx].set(top_gates)

        def expert_step(acc, ew):
            wi, wo, g = ew
            h = x @ wi.T
            a, b = jnp.split(h, 2, axis=-1)
            o = jax.nn.silu(a) * b @ wo.T
            return (acc + g[:, None] * o, None)
        acc, _ = jax.lax.scan(expert_step, jnp.zeros_like(x), (w_in, w_out, dense_gates.T))
        return acc.reshape(B, L, D) + bias
    x = L0_attn_inputs
    x = x + 0.5 * _L0_ffn_ref(_layernorm(x, axis=-1), L0_ffn_router_weight, L0_ffn_w_in, L0_ffn_w_out, L0_ffn_bias)
    x = x + _L0_attn_ref(_layernorm(x, axis=-1), L0_attn_w_q, L0_attn_w_k, L0_attn_w_v, L0_attn_w_o, L0_attn_b_o)
    x = x + 0.5 * _L0_ffn_ref(_layernorm(x, axis=-1), L0_ffn_router_weight, L0_ffn_w_in, L0_ffn_w_out, L0_ffn_bias)
    return x

_drawn_inputs = setup_inputs


def setup_inputs(seed=0):
    import zlib

    import numpy as np

    out = dict(_drawn_inputs(seed))
    spreads = {}
    factors = {'L0_attn_b_o': 2.732,
     'L0_ffn_router_weight': 3.912,
     'L0_ffn_w_in': 3.387,
     'L0_ffn_w_out': 3.394}
    for name, (base, spread) in spreads.items():
        noise = np.random.default_rng([zlib.crc32(name.encode()), seed]).standard_normal(out[name].shape)
        drawn = base * np.exp(spread * noise) if base else spread * noise
        out[name] = jnp.asarray(drawn.astype(out[name].dtype))
    for name, factor in factors.items():
        out[name] = (out[name] * factor).astype(out[name].dtype)
    return out
```

```python
from contextlib import ExitStack

import concourse.bass as bass
from concourse import mybir

ALU = mybir.AluOpType
ACT = mybir.ActivationFunctionType
F32 = mybir.dt.float32
F16 = mybir.dt.float16
BF16 = mybir.dt.bfloat16
I32 = mybir.dt.int32
AX_X = mybir.AxisListType.X

P = 128
BATCH, SEQ, D = 4, 256, 256
T = BATCH * SEQ
TILES = T // P
DK = D // P
E, TOPK, H = 8, 2, 512
HK = H // P
HEADS, HD = 16, 16
HPC = P // HD
VW = HD + 1
BLOCKS = (TOPK * T + E * (P - 1)) // P
EVEN, ODD = (BLOCKS + 1) // 2, BLOCKS // 2
PAIRS = TOPK * TILES
NEG = -1.0e30
AHEAD = 4
PEELED = 3
LOOPED = (BLOCKS - 2 - PEELED) // 2
AFTER = PEELED + 2 * LOOPED
EPS = 1e-5


def build(nc, x_in, wq_in, wk_in, wv_in, wo_in, bo_in, wr_in, win_in, wout_in, bias_in, out):
    with ExitStack() as ctx:
        def sb(name, shape, dt=F32):
            return ctx.enter_context(nc.sbuf_tensor(name, shape, dt))

        def sem(name):
            return ctx.enter_context(nc.semaphore(name))

        bank = [ctx.enter_context(nc.psum_tensor(f"bank{i}", [P, 512], F32)) for i in range(8)]

        xn_dram = nc.dram_tensor("xn_scratch", (T, D), F32, kind="Internal").ap()
        y_dram = nc.dram_tensor("y_scratch", (TOPK * T + BLOCKS * P, D), F32, kind="Internal").ap()

        w_in = sb("w_in", [P, E, DK, 2 * H])
        w_out = sb("w_out", [P, E, HK, D])
        wq, wk, wv, wo = (sb(n, [P, DK, D]) for n in ("wq", "wk", "wv", "wo"))
        wr = sb("wr", [P, DK, E])
        bias_half = sb("bias_half", [P, D])
        bo = sb("bo", [P, D])
        ident = sb("ident", [P, P])
        ident_b = sb("ident_b", [P, P], BF16)
        neg_mask = sb("neg_mask", [P, P], BF16)
        before = sb("before", [P, P], F16)
        ones = sb("ones", [P, P], F16)
        col = sb("col", [P, P])
        rev = sb("rev", [P, E])
        block_edge = sb("block_edge", [P, E])
        expert_before = sb("expert_before", [P, E, E])
        block_no = sb("block_no", [P, BLOCKS])
        pair_id = sb("pair_id", [P, PAIRS])
        trash_id = sb("trash_id", [P, BLOCKS])
        head_mask = sb("head_mask", [P, HPC])
        minus_half = sb("minus_half", [P, TILES])
        x = sb("x", [P, TILES, D])
        xn = sb("xn", [P, TILES, D])
        xnT = sb("xnT", [P, DK, T])
        stats = sb("stats", [P, TILES, 6])
        mv = sb("mv", [P, TILES, 2])
        var_eps = sb("var_eps", [P, TILES])
        rstd = sb("rstd", [P, TILES])
        logits = sb("logits", [P, TILES, E])
        logits2 = sb("logits2", [P, TILES, E])
        top = sb("top", [P, TOPK, TILES])
        hit = sb("hit", [P, TILES, E])
        first = sb("first", [P, TILES])
        choice = sb("choice", [P, TOPK, TILES, E])
        chosen = sb("chosen", [P, TILES, E], F16)
        gap = sb("gap", [P, TILES])
        e1 = sb("e1", [P, TILES])
        den = sb("den", [P, TILES])
        gate = sb("gate", [P, TOPK, TILES])
        over_edge = sb("over_edge", [P, E, E])
        n_blocks = sb("n_blocks", [P, E])
        first_block = sb("first_block", [P, E])
        end_block = sb("end_block", [P, E])
        place = sb("place", [P, TILES, E])
        placed = sb("placed", [P, TOPK, TILES, E])
        slot = sb("slot", [P, PAIRS])
        slot_i = sb("slot_i", [P, PAIRS], I32)
        row_i = sb("row_i", [P, PAIRS], I32)
        blk_i = sb("blk_i", [P, PAIRS], I32)
        row_hot = sb("row_hot", [P, PAIRS, P], F16)
        blk_hot = sb("blk_hot", [P, PAIRS, BLOCKS])
        blk_pair = sb("blk_pair", [P, PAIRS, BLOCKS], F16)
        pair_of = sb("pair_of", [P, BLOCKS])
        empty = sb("empty", [P, BLOCKS])
        wrap = sb("wrap", [P, BLOCKS])
        scatter_row = sb("scatter_row", [P, BLOCKS], I32)
        gather_row = sb("gather_row", [P, BLOCKS], I32)
        past = sb("past", [P, BLOCKS, E])
        block_expert_f = sb("block_expert_f", [P, BLOCKS])
        block_expert = sb("block_expert", [P, BLOCKS], I32)
        xb = [sb(f"xb{u}", [P, D]) for u in range(2)]
        xT = [sb(f"xT{u}", [P, DK, P]) for u in range(2)]
        sa = [sb(f"sa{u}", [P, H]) for u in range(2)]
        g = [sb(f"g{u}", [P, H]) for u in range(2)]
        gT = sb("gT", [P, HK, P])
        y = [sb(f"y{u}", [P, D]) for u in range(2)]
        y_in = sb("y_in", [P, TOPK, TILES, D])
        qT = sb("qT", [P, DK, SEQ])
        kT = sb("kT", [P, DK, SEQ])
        k_head = [sb(f"k_head{u}", [P, SEQ]) for u in range(4)]
        v = sb("v", [P, TILES, HEADS, VW])
        neg_max = [sb(f"neg_max{u}", [P, 2]) for u in range(4)]
        probs = [sb(f"probs{u}", [P, 3, P]) for u in range(3)]
        probsT = [sb(f"probsT{u}", [P, 3, P]) for u in range(2)]
        inv_sum = sb("inv_sum", [P, 2, HEADS])
        ctxv = sb("ctxv", [P, 2, HEADS, HD])
        ctxT = sb("ctxT", [P, DK, SEQ])

        x_loaded = [sem(f"x_loaded{i}") for i in range(2)]
        small_loaded = sem("small_loaded")
        attn_w_loaded = sem("attn_w_loaded")
        win_loaded = sem("win_loaded")
        xn_stored = sem("xn_stored")
        y_loaded = sem("y_loaded")
        out_stored = sem("out_stored")
        const_step = sem("const_step")
        const_ready = sem("const_ready")
        stats_done = sem("stats_done")
        mv_done = sem("mv_done")
        var_ready = sem("var_ready")
        rstd_ready = sem("rstd_ready")
        xn_ready = sem("xn_ready")
        xnT_in_psum = sem("xnT_in_psum")
        xnT_ready = sem("xnT_ready")
        bias_added = sem("bias_added")
        x_added = sem("x_added")
        logits_done = sem("logits_done")
        route_step = sem("route_step")
        chosen_ready = sem("chosen_ready")
        gap_ready = sem("gap_ready")
        e1_ready = sem("e1_ready")
        ranks_done = sem("ranks_done")
        hot_ready = sem("hot_ready")
        pairs_done = sem("pairs_done")
        plan_ready = sem("plan_ready")
        gathered = [sem(f"gathered{u}") for u in range(2)]
        xT_in_psum = sem("xT_in_psum")
        xT_ready = sem("xT_ready")
        a_done = sem("a_done")
        b_done = sem("b_done")
        silu_done = sem("silu_done")
        g_done = sem("g_done")
        gT_in_psum = sem("gT_in_psum")
        gT_ready = sem("gT_ready")
        y_done = sem("y_done")
        y_copied = sem("y_copied")
        scattered = [sem(f"scattered{u}") for u in range(2)]
        v_done = sem("v_done")
        v_ready = sem("v_ready")
        q_done = sem("q_done")
        k_done = sem("k_done")
        q_ready = sem("q_ready")
        k_ready = sem("k_ready")
        k_head_ready = sem("k_head_ready")
        scores_done = sem("scores_done")
        max_done = sem("max_done")
        probs_ready = sem("probs_ready")
        probsT_done = sem("probsT_done")
        probsT_even = sem("probsT_even")
        probsT_odd = sem("probsT_odd")
        pv_done = sem("pv_done")
        inv_ready = sem("inv_ready")
        ctx_ready = sem("ctx_ready")
        ctxT_done = sem("ctxT_done")
        ctxT_ready = sem("ctxT_ready")
        o_done = sem("o_done")
        attn_added = sem("attn_added")

        block = ctx.enter_context(nc.Block())

        def after_first(f, j, n):
            return f or not isinstance(j, int) or j >= n

        def bc(ap, axis, shape):
            return ap.unsqueeze(axis).to_broadcast(shape)

        x_rows = x_in.rearrange("b (j p) d -> p (b j) d", p=P)
        out_rows = out.rearrange("b (j p) d -> p (b j) d", p=P)
        xn_rows = xn_dram.rearrange("(i p) d -> p i d", p=P)
        y_rows = y_dram[0:TOPK * T, :].rearrange("(k i p) d -> p k i d", p=P, k=TOPK)

        @block.sync
        def _(sp):
            for half in range(2):
                rows = slice(half * TILES // 2, (half + 1) * TILES // 2)
                sp.dma_start(x[:, rows, :], x_rows[:, rows, :]).then_inc(x_loaded[half], 16)
            sp.dma_start(wr[:, :, :], wr_in.rearrange("(k p) e -> p k e", p=P)).then_inc(small_loaded, 16)
            sp.dma_start(bias_half[:, :], bias_in.partition_broadcast(P)).then_inc(small_loaded, 16)
            sp.dma_start(bo[:, :], bo_in.partition_broadcast(P)).then_inc(small_loaded, 16)
            for e in range(E):
                sp.dma_start(w_in[:, e, :, :], win_in[e].rearrange("(k p) n -> p k n", p=P)).then_inc(win_loaded, 16)
                sp.dma_start(w_out[:, e, :, :], wout_in[e].rearrange("(k p) n -> p k n", p=P)).then_inc(win_loaded, 16)
            for dst, src in ((wq, wq_in), (wk, wk_in), (wv, wv_in), (wo, wo_in)):
                sp.dma_start(dst[:, :, :], src.rearrange("(k p) n -> p k n", p=P)).then_inc(attn_w_loaded, 16)
            for f in range(2):
                sp.wait_ge(xn_ready, TILES * (2 * f + 1))
                sp.dma_start(xn_rows, xn[:, :, :]).then_inc(xn_stored, 16)
                sp.wait_ge(scattered[0], 16 * EVEN * (f + 1))
                sp.wait_ge(scattered[1], 16 * ODD * (f + 1))
                for i in range(0, TILES, 2):
                    for k in range(TOPK):
                        sp.dma_start(y_in[:, k, i:i + 2, :], y_rows[:, k, i:i + 2, :]).then_inc(y_loaded, 16)
            for i in range(0, TILES, 2):
                sp.wait_ge(x_added, TILES + i + 2)
                sp.dma_start(out_rows[:, i:i + 2, :], x[:, i:i + 2, :]).then_inc(out_stored, 16)
            sp.wait_ge(out_stored, 16 * TILES // 2)

        @block.gpsimd
        def _(pool):
            steps = [0]

            def then(ins):
                steps[0] += 1
                ins.then_inc(const_step, 1)
                pool.wait_ge(const_step, steps[0])

            def iota(t, pattern, base, mult):
                then(pool.iota(t, pattern, base=base, channel_multiplier=mult, allow_small_or_imprecise_dtypes=True))

            def select(t, pattern, base, mult, op, fill):
                then(pool.affine_select(out=t, in_=t, pattern=pattern, compare_op=op, fill=fill, base=base,
                                        channel_multiplier=mult))

            then(pool.memset(ident[:, :], 0.0))
            select(ident[:, :], [[-1, P]], 0, 1, ALU.not_equal, 1.0)
            then(pool.memset(minus_half[:, :], -0.5))
            iota(rev[:, :], [[-1, E]], E, 0)
            then(pool.memset(ones[:, :], 1.0))
            then(pool.memset(before[:, :], 1.0))
            select(before[:, :], [[1, P]], 0, -1, ALU.is_gt, 0.0)
            iota(block_edge[:, :], [[P, E]], 0, 0)
            then(pool.memset(expert_before[:, :, :], 1.0))
            select(expert_before[:, :, :], [[1, E], [-1, E]], 0, 0, ALU.is_gt, 0.0)
            iota(col[:, :], [[1, P]], 0, 0)
            iota(block_no[:, :], [[1, BLOCKS]], 0, 0)
            iota(pair_id[:, :].rearrange("p (k i) -> p k i", k=TOPK), [[T, TOPK], [P, TILES]], 1, 1)
            iota(trash_id[:, :], [[P, BLOCKS]], TOPK * T + 1, 1)
            then(pool.memset(neg_mask[:, :], 0.0))
            select(neg_mask[:, :], [[-1, P]], 0, 1, ALU.is_ge, NEG)
            then(pool.tensor_copy(ident_b[:, :], ident[:, :]))
            then(pool.memset(head_mask[:, :], 1.0))
            select(head_mask[:, :], [[-HD, HPC]], 0, 1, ALU.is_ge, 0.0)
            select(head_mask[:, :], [[HD, HPC]], HD - 1, -1, ALU.is_ge, 0.0)
            pool.memset(v[:, :, :, HD:VW], 1.0).then_inc(const_ready, 1)
            pool.wait_ge(small_loaded, 48)
            then(pool.tensor_scalar(bias_half[:, :], bias_half[:, :], 0.5, None, ALU.mult))

            def inverse_root(phase):
                pool.wait_ge(var_ready, phase + 1)
                pool.tensor_tensor(rstd[:, :], var_eps[:, :], minus_half[:, :], ALU.pow).then_inc(rstd_ready, 1)

            def add_bias(phase, b):
                pool.wait_ge(xn_ready, TILES * (phase + 1))
                pool.tensor_tensor(x[:, :, :], x[:, :, :], bc(b[:, :], 1, [P, TILES, D]), ALU.add)\
                    .then_inc(bias_added, 1)

            def gather(f, j):
                if f or j >= 2:
                    pool.wait_ge(xT_in_psum, f * BLOCKS + max(j - 1, 0))
                pool.indirect_dma_start(out=xb[j % 2][:, :], out_offset=None, in_=xn_dram,
                                        in_offset=bass.IndirectOffsetOnAxis(ap=gather_row[:, j:j + 1], axis=0))\
                    .then_inc(gathered[j % 2], 16)

            def scatter(f, j):
                pool.wait_ge(y_copied, f * BLOCKS + j + 1)
                pool.indirect_dma_start(out=y_dram, in_=y[j % 2][:, :], in_offset=None,
                                        out_offset=bass.IndirectOffsetOnAxis(ap=scatter_row[:, j:j + 1], axis=0))\
                    .then_inc(scattered[j % 2], 16)

            def ffn(f):
                inverse_root(2 * f)
                add_bias(2 * f, bias_half)
                pool.wait_ge(plan_ready, f + 1)
                pool.wait_ge(xn_stored, 16 * (f + 1))
                if f:
                    pool.wait_ge(y_loaded, 16 * TILES * f)
                for j in range(AHEAD):
                    gather(f, j)
                for j in range(BLOCKS):
                    if j + AHEAD < BLOCKS:
                        gather(f, j + AHEAD)
                    scatter(f, j)

            ffn(0)
            inverse_root(1)
            add_bias(1, bo)

            with pool.Fori(0, BATCH) as b:
                pool.wait_ge(k_ready, b + 1)
                for h in range(HEADS):
                    if h >= 4:
                        pool.wait_ge(scores_done, b * HEADS + (h - 3))
                    pool.tensor_tensor(k_head[h % 4][:, :], kT[:, h // HPC, :],
                                       head_mask[:, h % HPC:h % HPC + 1].to_broadcast([P, SEQ]), ALU.mult).then_inc(k_head_ready, 1)
            ffn(1)

        @block.scalar
        def _(act):
            def turn_out(phase):
                for pair in range(TILES // 2):
                    act.wait_ge(xnT_in_psum, 4 * phase + pair + 1)
                    act.activation(xnT[:, :, pair * 256:(pair + 1) * 256],
                                   bank[pair % 2][:, :].rearrange("p (k t) -> p k t", k=DK), ACT.Copy)\
                        .then_inc(xnT_ready, 1)

            def copy_xT(f, j, u):
                act.wait_ge(xT_in_psum, f * BLOCKS + j + 1)
                if after_first(f, j, 2):
                    act.wait_ge(b_done, f * BLOCKS + j - 1)
                act.activation(xT[u][:, :, :], bank[5][:, 0:D].rearrange("p (k t) -> p k t", k=DK), ACT.Copy)\
                    .then_inc(xT_ready, 1)

            def silu(f, j, u):
                act.wait_ge(a_done, f * BLOCKS + j + 1)
                if after_first(f, j, 2):
                    act.wait_ge(g_done, f * BLOCKS + j - 1)
                act.activation(sa[u][:, :], bank[u][:, :], ACT.Silu).then_inc(silu_done, 1)

            def copy_y(f, j, u, scatters_before):
                act.wait_ge(y_done, f * BLOCKS + j + 1)
                if not isinstance(scatters_before, int) or scatters_before:
                    act.wait_ge(scattered[u], scatters_before * 16)
                act.activation(y[u][:, :], bank[6][:, 0:D], ACT.Copy).then_inc(y_copied, 1)

            def ffn(f):
                turn_out(2 * f)
                act.wait_ge(gap_ready, f + 1)
                act.activation(e1[:, :], gap[:, :], ACT.Exp).then_inc(e1_ready, 1)
                base = (EVEN * f, ODD * f)
                copy_xT(f, 0, 0)
                silu(f, 0, 0)
                copy_xT(f, 1, 1)

                def body(j, u, of_parity, silu_next=True, copy_next=True):
                    if silu_next:
                        silu(f, j + 1, 1 - u)
                    if copy_next:
                        copy_xT(f, j + 2, u)
                    copy_y(f, j, u, of_parity + base[u])

                for j in range(PEELED):
                    body(j, j % 2, j // 2)
                with act.Fori(0, LOOPED) as i:
                    for u in range(2):
                        body(i * 2 + (PEELED + u), (PEELED + u) % 2, i + (PEELED + u) // 2)
                for j in range(AFTER, BLOCKS):
                    body(j, j % 2, j // 2, j + 1 < BLOCKS, j + 2 < BLOCKS)

            ffn(0)
            turn_out(1)
            act.wait_ge(const_ready, 1)
            for t in range(TILES):
                act.wait_ge(v_done, t + 1)
                act.activation(v[:, t, :, 0:HD], bank[t % 3][:, 0:D].rearrange("p (h d) -> p h d", h=HEADS), ACT.Copy)\
                    .then_inc(v_ready, 1)
            with act.Fori(0, BATCH) as b:
                act.wait_ge(q_done, b + 1)
                act.activation(qT[:, :, :], bank[7][:, :].rearrange("p (k t) -> p k t", k=DK), ACT.Copy,
                               scale=1.0 / SEQ ** 0.5).then_inc(q_ready, 1)
                for t in range(HEADS + 2):
                    if t < HEADS:
                        act.wait_ge(max_done, b * HEADS + (t + 1))
                        if t >= 3:
                            act.wait_ge(probsT_done, b * HEADS + (t - 2))
                        act.activation(probs[t % 3][:, 0, :], bank[t % 3][:, 0:P], ACT.Exp,
                                       bias=neg_max[t % 4][:, 0:1])
                        act.activation(probs[t % 3][:, 1:3, :], bank[t % 3][:, P:3 * P].rearrange("p (k t) -> p k t", k=2),
                                       ACT.Exp, bias=neg_max[t % 4][:, 1:2]).then_inc(probs_ready, 1)
                    if t >= 2 and t % 2:
                        h = t - 2
                        act.wait_ge(probsT_done, b * HEADS + (h + 1))
                        if h >= 2:
                            act.wait_ge(pv_done, b * HEADS + (h - 1))
                        act.activation(probsT[1][:, :, :], bank[4][:, 0:3 * P].rearrange("p (k t) -> p k t", k=3),
                                       ACT.Copy).then_inc(probsT_odd, 1)
                act.wait_ge(ctxT_done, b + 1)
                act.activation(ctxT[:, :, :], bank[7][:, :].rearrange("p (k t) -> p k t", k=DK), ACT.Copy)\
                    .then_inc(ctxT_ready, 1)
            ffn(1)

        @block.vector
        def _(dve):
            steps = [0]

            def then(ins):
                steps[0] += 1
                ins.then_inc(route_step, 1)
                dve.wait_ge(route_step, steps[0])

            def normalise(phase):
                for i in range(TILES):
                    if phase == 0 and i % (TILES // 2) == 0:
                        dve.wait_ge(x_loaded[i // (TILES // 2)], 16)
                    last = dve.bn_stats(stats[:, i, :], x[:, i, :])
                last.then_inc(stats_done, 1)
                dve.wait_ge(stats_done, phase + 1)
                for i in range(TILES):
                    last = dve.bn_aggr(mv[:, i, :], stats[:, i, :])
                last.then_inc(mv_done, 1)
                dve.wait_ge(mv_done, phase + 1)
                dve.tensor_scalar(var_eps[:, :], mv[:, :, 1], EPS, None, ALU.add).then_inc(var_ready, 1)
                dve.wait_ge(rstd_ready, phase + 1)
                if phase:
                    dve.wait_ge(xnT_in_psum, 4 * phase)
                for i in range(TILES):
                    dve.tensor_scalar(xn[:, i, :], x[:, i, :], mv[:, i, 0:1], rstd[:, i:i + 1], ALU.subtract, ALU.mult)\
                        .then_inc(xn_ready, 1)

            def route(f):
                te = [P, TILES, E]
                dve.wait_ge(logits_done, f + 1)
                then(dve.tensor_copy(logits[:, :, :], bank[7][:, 0:TILES * E].rearrange("p (i e) -> p i e", e=E)))
                for k, values in enumerate((logits, logits2)):
                    then(dve.tensor_reduce(top[:, k, :], values[:, :, :], AX_X, ALU.max))
                    then(dve.tensor_tensor(hit[:, :, :], values[:, :, :], bc(top[:, k, :], 2, te), ALU.is_equal))
                    then(dve.tensor_tensor(hit[:, :, :], hit[:, :, :], bc(rev[:, :], 1, te), ALU.mult))
                    then(dve.tensor_reduce(first[:, :], hit[:, :, :], AX_X, ALU.max))
                    then(dve.tensor_tensor(choice[:, k, :, :], bc(rev[:, :], 1, te), bc(first[:, :], 2, te), ALU.is_equal))
                    if k == 0:
                        then(dve.scalar_tensor_tensor(logits2[:, :, :], choice[:, 0, :, :], -3.0e38, logits[:, :, :],
                                                      ALU.mult, ALU.add))
                dve.tensor_tensor(chosen[:, :, :], choice[:, 0, :, :], choice[:, 1, :, :], ALU.add).then_inc(chosen_ready, 1)
                dve.tensor_tensor(gap[:, :], top[:, 1, :], top[:, 0, :], ALU.subtract).then_inc(gap_ready, 1)
                dve.wait_ge(ranks_done, f + 1)
                then(dve.tensor_tensor(over_edge[:, :, :], bc(bank[6][:, 0:E], 2, [P, E, E]),
                                       bc(block_edge[:, :], 1, [P, E, E]), ALU.is_gt))
                then(dve.tensor_reduce(n_blocks[:, :], over_edge[:, :, :], AX_X, ALU.add))
                then(dve.tensor_tensor(over_edge[:, :, :], expert_before[:, :, :], bc(n_blocks[:, :], 1, [P, E, E]), ALU.mult))
                then(dve.tensor_reduce(first_block[:, :], over_edge[:, :, :], AX_X, ALU.add))
                then(dve.tensor_tensor(end_block[:, :], first_block[:, :], n_blocks[:, :], ALU.add))
                then(dve.scalar_tensor_tensor(place[:, :, :], bc(first_block[:, :], 1, te), float(P),
                                              bank[4][:, 0:TILES * E].rearrange("p (i e) -> p i e", e=E),
                                              ALU.mult, ALU.add))
                for k in range(TOPK):
                    then(dve.tensor_tensor(placed[:, k, :, :], choice[:, k, :, :], place[:, :, :], ALU.mult))
                then(dve.tensor_reduce(slot[:, :].rearrange("p (k i) -> p k i", k=TOPK), placed[:, :, :, :], AX_X, ALU.add))
                then(dve.tensor_copy(slot_i[:, :], slot[:, :]))
                then(dve.tensor_scalar(row_i[:, :], slot_i[:, :], P - 1, None, ALU.bitwise_and))
                then(dve.tensor_scalar(blk_i[:, :], slot_i[:, :], 7, None, ALU.logical_shift_right))
                then(dve.tensor_tensor(blk_hot[:, :, :], bc(blk_i[:, :], 2, [P, PAIRS, BLOCKS]),
                                       bc(block_no[:, :], 1, [P, PAIRS, BLOCKS]), ALU.is_equal))
                then(dve.tensor_tensor(blk_pair[:, :, :], blk_hot[:, :, :], bc(pair_id[:, :], 2, [P, PAIRS, BLOCKS]), ALU.mult))
                dve.tensor_tensor(row_hot[:, :, :], bc(row_i[:, :], 2, [P, PAIRS, P]), bc(col[:, :], 1, [P, PAIRS, P]),
                                  ALU.is_equal).then_inc(hot_ready, 1)
                then(dve.tensor_tensor(past[:, :, :], bc(end_block[:, :], 1, [P, BLOCKS, E]),
                                       bc(block_no[:, :], 2, [P, BLOCKS, E]), ALU.is_le))
                then(dve.tensor_reduce(block_expert_f[:, :], past[:, :, :], AX_X, ALU.add))
                then(dve.tensor_scalar(block_expert[:, :], block_expert_f[:, :], float(E - 1), None, ALU.min))
                dve.wait_ge(pairs_done, f + 1)
                then(dve.tensor_copy(pair_of[:, :], bank[7][:, 0:BLOCKS]))
                then(dve.scalar_tensor_tensor(empty[:, :], pair_of[:, :], 0.0, trash_id[:, :], ALU.is_equal, ALU.mult))
                then(dve.scalar_tensor_tensor(scatter_row[:, :], pair_of[:, :], 1.0, empty[:, :], ALU.subtract, ALU.add))
                then(dve.tensor_scalar(wrap[:, :], pair_of[:, :], T + 0.5, -float(T), ALU.is_gt, ALU.mult))
                then(dve.scalar_tensor_tensor(wrap[:, :], pair_of[:, :], 1.0, wrap[:, :], ALU.subtract, ALU.add))
                dve.tensor_scalar(gather_row[:, :], wrap[:, :], 0.0, None, ALU.max).then_inc(plan_ready, 1)
                dve.wait_ge(e1_ready, f + 1)
                then(dve.tensor_scalar(den[:, :], e1[:, :], 1.0, None, ALU.add))
                then(dve.reciprocal(den[:, :], den[:, :]))
                then(dve.tensor_scalar(gate[:, 0, :], den[:, :], 0.5, None, ALU.mult))
                then(dve.tensor_tensor(gate[:, 1, :], gate[:, 0, :], e1[:, :], ALU.mult))

            def gated(f, j, u):
                dve.wait_ge(b_done, f * BLOCKS + j + 1)
                dve.wait_ge(silu_done, f * BLOCKS + j + 1)
                if after_first(f, j, 2):
                    dve.wait_ge(gT_in_psum, f * BLOCKS + j - 1)
                dve.tensor_tensor(g[u][:, :], sa[u][:, :], bank[2 + u][:, :], ALU.mult).then_inc(g_done, 1)

            def copy_gT(f, j):
                dve.wait_ge(gT_in_psum, f * BLOCKS + j + 1)
                if after_first(f, j, 1):
                    dve.wait_ge(y_done, f * BLOCKS + j)
                dve.tensor_copy(gT[:, :, :], bank[4][:, :].rearrange("p (c t) -> p c t", c=HK)).then_inc(gT_ready, 1)

            def ffn(f):
                normalise(2 * f)
                route(f)
                gated(f, 0, 0)
                for j in range(PEELED):
                    copy_gT(f, j)
                    gated(f, j + 1, 1 - j % 2)
                with dve.Fori(0, LOOPED) as i:
                    for u in range(PEELED, PEELED + 2):
                        copy_gT(f, i * 2 + u)
                        gated(f, i * 2 + (u + 1), 1 - u % 2)
                for j in range(AFTER, BLOCKS):
                    copy_gT(f, j)
                    if j + 1 < BLOCKS:
                        gated(f, j + 1, 1 - j % 2)
                dve.wait_ge(bias_added, 2 * f + 1)
                dve.wait_ge(y_loaded, 16 * TILES * (f + 1))
                for i in range(TILES):
                    then(dve.scalar_tensor_tensor(x[:, i, :], y_in[:, 0, i, :], gate[:, 0, i:i + 1], x[:, i, :],
                                                  ALU.mult, ALU.add))
                    ins = dve.scalar_tensor_tensor(x[:, i, :], y_in[:, 1, i, :], gate[:, 1, i:i + 1], x[:, i, :],
                                                   ALU.mult, ALU.add)
                    ins.then_inc(x_added, 1)
                dve.wait_ge(x_added, TILES * (f + 1))

            ffn(0)
            normalise(1)
            dve.wait_ge(bias_added, 2)
            with dve.Fori(0, BATCH) as b:
                dve.wait_ge(k_done, b + 1)
                dve.tensor_copy(kT[:, :, :], bank[3][:, :].rearrange("p (k t) -> p k t", k=DK)).then_inc(k_ready, 1)
                for t in range(HEADS + 2):
                    if t < HEADS:
                        dve.wait_ge(scores_done, b * HEADS + (t + 1))
                        if t >= 4:
                            dve.wait_ge(probs_ready, b * HEADS + (t - 3))
                        dve.tensor_reduce(neg_max[t % 4][:, 0:1], bank[t % 3][:, 0:P], AX_X, ALU.max, negate=True)
                        dve.tensor_reduce(neg_max[t % 4][:, 1:2], bank[t % 3][:, P:3 * P], AX_X, ALU.max, negate=True)\
                            .then_inc(max_done, 1)
                    if t >= 2 and t % 2 == 0:
                        h = t - 2
                        dve.wait_ge(probsT_done, b * HEADS + (h + 1))
                        if h >= 2:
                            dve.wait_ge(pv_done, b * HEADS + (h - 1))
                        dve.tensor_copy(probsT[0][:, :, :], bank[3][:, 0:3 * P].rearrange("p (k t) -> p k t", k=3))\
                            .then_inc(probsT_even, 1)
                dve.wait_ge(pv_done, b * HEADS + HEADS)
                for qt in range(2):
                    cv = bank[5 + qt][:, 0:HEADS * VW].rearrange("p (h w) -> p h w", w=VW)
                    ins = dve.reciprocal(inv_sum[:, qt, :], cv[:, :, HD])
                ins.then_inc(inv_ready, 1)
                dve.wait_ge(inv_ready, b + 1)
                for qt in range(2):
                    cv = bank[5 + qt][:, 0:HEADS * VW].rearrange("p (h w) -> p h w", w=VW)
                    ins = dve.tensor_tensor(ctxv[:, qt, :, :], cv[:, :, 0:HD], bc(inv_sum[:, qt, :], 2, [P, HEADS, HD]),
                                            ALU.mult)
                ins.then_inc(ctx_ready, 1)
                dve.wait_ge(o_done, b + 1)
                rows = x[:, bass.ds(b * 2, 2), :]
                dve.tensor_tensor(rows, rows, bank[5][:, :].rearrange("p (q d) -> p q d", q=2), ALU.add)\
                    .then_inc(attn_added, 1)
            dve.wait_ge(attn_added, BATCH)
            ffn(1)

        @block.tensor
        def _(pe):
            def turn(phase):
                for pair in range(TILES // 2):
                    pe.wait_ge(xn_ready, TILES * phase + 2 * pair + 2)
                    if pair >= 2:
                        pe.wait_ge(xnT_ready, 4 * phase + pair - 1)
                    for k in range(DK):
                        for i in range(2):
                            at = k * 256 + i * P
                            last = pe.transpose(bank[pair % 2][:, at:at + P], xn[:, 2 * pair + i, k * P:(k + 1) * P],
                                                ident[:, :])
                    last.then_inc(xnT_in_psum, 1)

            def route(f):
                for i in range(TILES):
                    if i % 2 == 0:
                        pe.wait_ge(xnT_ready, 8 * f + i // 2 + 1)
                    for k in range(DK):
                        last = pe.matmul(bank[7][:, i * E:(i + 1) * E], xnT[:, k, i * P:(i + 1) * P], wr[:, k, :],
                                         start=(k == 0), stop=(k == DK - 1))
                last.then_inc(logits_done, 1)
                pe.wait_ge(chosen_ready, f + 1)
                flat = chosen[:, :, :].rearrange("p i e -> p (i e)")
                pe.matmul(bank[4][:, 0:TILES * E], before[:, :], flat, start=True, stop=False, skip_group_check=True)
                for i in range(TILES - 1):
                    left = TILES - 1 - i
                    pe.matmul(bank[4][:, (i + 1) * E:TILES * E].rearrange("p (i e) -> p i e", e=E), ones[:, :],
                              bc(chosen[:, i, :], 1, [P, left, E]), start=False, stop=(left == 1), skip_group_check=True)
                for i in range(TILES):
                    last = pe.matmul(bank[6][:, 0:E], ones[:, :], chosen[:, i, :], start=(i == 0), stop=(i == TILES - 1))
                last.then_inc(ranks_done, 1)
                pe.wait_ge(hot_ready, f + 1)
                for q in range(PAIRS):
                    last = pe.matmul(bank[7][:, 0:BLOCKS], row_hot[:, q, :], blk_pair[:, q, :], start=(q == 0),
                                     stop=(q == PAIRS - 1))
                last.then_inc(pairs_done, 1)

            def turn_block(f, j, u, gathers):
                pe.wait_ge(gathered[u], gathers * 16)
                if after_first(f, j, 1):
                    pe.wait_ge(xT_ready, f * BLOCKS + j)
                for k in range(DK):
                    last = pe.transpose(bank[5][:, k * P:(k + 1) * P], xb[u][:, k * P:(k + 1) * P], ident[:, :])
                last.then_inc(xT_in_psum, 1)

            def expert(j):
                return pe.value_load(block_expert[0:1, bass.ds(j, 1)], min_val=0, max_val=E - 1)

            def project(f, j, u, half):
                e = expert(j)
                if half == 0:
                    pe.wait_ge(xT_ready, f * BLOCKS + j + 1)
                    if after_first(f, j, 2):
                        pe.wait_ge(silu_done, f * BLOCKS + j - 1)
                else:
                    if after_first(f, j, 2):
                        pe.wait_ge(g_done, f * BLOCKS + j - 1)
                for k in range(DK):
                    last = pe.matmul(bank[2 * half + u][:, :], xT[u][:, k, :],
                                     w_in[:, bass.ds(e, 1), k, half * H:(half + 1) * H],
                                     start=(k == 0), stop=(k == DK - 1))
                last.then_inc(b_done if half else a_done, 1)

            def turn_gated(f, j, u):
                pe.wait_ge(g_done, f * BLOCKS + j + 1)
                if after_first(f, j, 1):
                    pe.wait_ge(gT_ready, f * BLOCKS + j)
                for c in range(HK):
                    last = pe.transpose(bank[4][:, c * P:(c + 1) * P], g[u][:, c * P:(c + 1) * P], ident[:, :])
                last.then_inc(gT_in_psum, 1)

            def combine(f, j):
                e = expert(j)
                pe.wait_ge(gT_ready, f * BLOCKS + j + 1)
                if after_first(f, j, 1):
                    pe.wait_ge(y_copied, f * BLOCKS + j)
                for c in range(HK):
                    last = pe.matmul(bank[6][:, 0:D], gT[:, c, :], w_out[:, bass.ds(e, 1), c, :], start=(c == 0),
                                     stop=(c == HK - 1))
                last.then_inc(y_done, 1)

            def ffn(f):
                turn(2 * f)
                if f == 0:
                    pe.wait_ge(small_loaded, 48)
                route(f)
                pe.wait_ge(plan_ready, f + 1)
                pe.wait_ge(win_loaded, 32 * E)
                base = (EVEN * f, ODD * f)
                turn_block(f, 0, 0, base[0] + 1)
                project(f, 0, 0, 0)
                project(f, 0, 0, 1)
                turn_block(f, 1, 1, base[1] + 1)

                def body(j, u, of_parity, project_next=True, turn_next=True):
                    if project_next:
                        project(f, j + 1, 1 - u, 0)
                    turn_gated(f, j, u)
                    if project_next:
                        project(f, j + 1, 1 - u, 1)
                    if turn_next:
                        turn_block(f, j + 2, u, of_parity + (base[u] + 2))
                    combine(f, j)

                for j in range(PEELED):
                    body(j, j % 2, j // 2)
                with pe.Fori(0, LOOPED) as i:
                    for u in range(2):
                        body(i * 2 + (PEELED + u), (PEELED + u) % 2, i + (PEELED + u) // 2)
                for j in range(AFTER, BLOCKS):
                    body(j, j % 2, j // 2, j + 1 < BLOCKS, j + 2 < BLOCKS)

            pe.wait_ge(const_step, 2)
            pe.wait_ge(const_ready, 1)
            ffn(0)
            turn(1)
            pe.wait_ge(attn_w_loaded, 64)
            pe.wait_ge(xnT_ready, 8)
            for t in range(TILES):
                if t >= 3:
                    pe.wait_ge(v_ready, t - 2)
                for k in range(DK):
                    last = pe.matmul(bank[t % 3][:, 0:D], xnT[:, k, t * P:(t + 1) * P], wv[:, k, :], start=(k == 0),
                                     stop=(k == DK - 1))
                last.then_inc(v_done, 1)
            pe.wait_ge(v_ready, TILES)
            with pe.Fori(0, BATCH) as b:
                for w, to, signal in ((wq, bank[7], q_done), (wk, bank[3], k_done)):
                    for c in range(DK):
                        for k in range(DK):
                            last = pe.matmul(to[:, c * SEQ:(c + 1) * SEQ], w[:, k, c * P:(c + 1) * P],
                                             xnT[:, k, bass.ds(b * SEQ, SEQ)], start=(k == 0), stop=(k == DK - 1))
                    last.then_inc(signal, 1)
                pe.wait_ge(q_ready, b + 1)
                for t in range(HEADS + 3):
                    if t < HEADS:
                        c = t // HPC
                        s = bank[t % 3]
                        pe.wait_ge(k_head_ready, b * HEADS + (t + 1))
                        if t >= 3:
                            pe.wait_ge(probs_ready, b * HEADS + (t - 2))
                        pe.matmul(s[:, 0:P], qT[:, c, 0:P], k_head[t % 4][:, 0:P], start=True, stop=False)
                        pe.matmul(s[:, 0:P], ident_b[:, :], neg_mask[:, :], start=False, stop=True)
                        pe.matmul(s[:, P:3 * P], qT[:, c, P:SEQ], k_head[t % 4][:, :], start=True, stop=False)
                        pe.matmul(s[:, 2 * P:3 * P], ident_b[:, :], neg_mask[:, :], start=False, stop=True)\
                            .then_inc(scores_done, 1)
                    if 2 <= t < HEADS + 2:
                        h = t - 2
                        pe.wait_ge(probs_ready, b * HEADS + (h + 1))
                        if h < 2:
                            pe.wait_ge(k_ready, b + 1)
                        if h >= 2:
                            pe.wait_ge(probsT_odd if h % 2 else probsT_even, b * (HEADS // 2) + h // 2)
                        for i in range(3):
                            last = pe.transpose(bank[3 + h % 2][:, i * P:(i + 1) * P], probs[h % 3][:, i, :], ident[:, :])
                        last.then_inc(probsT_done, 1)
                    if t >= 3:
                        h = t - 3
                        pr = probsT[h % 2]
                        if h % 2:
                            pe.wait_ge(probsT_odd, b * (HEADS // 2) + h // 2 + 1)
                        else:
                            pe.wait_ge(probsT_even, b * (HEADS // 2) + h // 2 + 1)
                        at = slice(h * VW, (h + 1) * VW)
                        v0, v1 = v[:, bass.ds(b * 2, 1), h, :], v[:, bass.ds(b * 2 + 1, 1), h, :]
                        pe.matmul(bank[5][:, at], pr[:, 0, :], v0, start=True, stop=True)
                        pe.matmul(bank[6][:, at], pr[:, 1, :], v0, start=True, stop=False)
                        pe.matmul(bank[6][:, at], pr[:, 2, :], v1, start=False, stop=True).then_inc(pv_done, 1)
                pe.wait_ge(ctx_ready, b + 1)
                for c in range(DK):
                    for qt in range(2):
                        heads = ctxv[:, qt, c * HPC:(c + 1) * HPC, :].rearrange("p h d -> p (h d)")
                        last = pe.transpose(bank[7][:, c * SEQ + qt * P:c * SEQ + (qt + 1) * P], heads, ident[:, :])
                last.then_inc(ctxT_done, 1)
                pe.wait_ge(ctxT_ready, b + 1)
                for qt in range(2):
                    for c in range(DK):
                        last = pe.matmul(bank[5][:, qt * D:(qt + 1) * D], ctxT[:, c, qt * P:(qt + 1) * P], wo[:, c, :],
                                         start=(c == 0), stop=(c == DK - 1))
                last.then_inc(o_done, 1)
            ffn(1)


def kernel(**inputs):
    import numpy as np
    import concourse.bacc as bacc
    from concourse.bass_utils import run_bass_kernel_spmd

    def lay(name, turned=False):
        a = np.asarray(inputs[name])
        return np.ascontiguousarray(np.swapaxes(a, -1, -2) if turned else a)

    arrays = {
        "x": lay("L0_attn_inputs"),
        "wq_t": lay("L0_attn_w_q", True),
        "wk_t": lay("L0_attn_w_k", True),
        "wv_t": lay("L0_attn_w_v", True),
        "wo_t": lay("L0_attn_w_o", True),
        "bo": lay("L0_attn_b_o"),
        "wr_t": lay("L0_ffn_router_weight", True),
        "win_t": lay("L0_ffn_w_in", True),
        "wout_t": lay("L0_ffn_w_out", True),
        "bias": lay("L0_ffn_bias"),
    }
    nc = bacc.Bacc("TRN2", target_bir_lowering=False, num_devices=1)
    ins = [nc.dram_tensor(f"in_{n}", a.shape, F32, kind="ExternalInput").ap() for n, a in arrays.items()]
    out = nc.dram_tensor("out", (BATCH, SEQ, D), F32, kind="ExternalOutput").ap()
    build(nc, *ins, out)
    return run_bass_kernel_spmd(nc, [{f"in_{n}": a for n, a in arrays.items()}], core_ids=[0]).results[0]["out"]
```

```python
from contextlib import ExitStack

import numpy as np

import concourse.bass as bass
from concourse import mybir

ALU = mybir.AluOpType
ACT = mybir.ActivationFunctionType
F32 = mybir.dt.float32
F16 = mybir.dt.float16
BF16 = mybir.dt.bfloat16
I32 = mybir.dt.int32
F32R = mybir.dt.float32r
AX_X = mybir.AxisListType.X

P = 128
BATCH, SEQ, D = 4, 256, 256
T = BATCH * SEQ
TILES = T // P
DK = D // P
E, TOPK, H = 8, 2, 512
HK = H // P
HEADS, HD = 16, 16
HPC = P // HD
HPAIRS = HEADS // 2
CPAIRS = HPC // 2
SLAG = 2
BLOCKS = (TOPK * T + E * (P - 1)) // P
EVEN, ODD = (BLOCKS + 1) // 2, BLOCKS // 2
PAIRS = TOPK * TILES
NEG = -1.0e30
AHEAD = 4
PEELED = 3
LOOPED = (BLOCKS - 2 - PEELED) // 2
AFTER = PEELED + 2 * LOOPED
STAGES = 3
CONSTS = 20
KSLOTS = 2
P_SCALE = 2.0 ** 15
VBANK = (0, 1, 3, 4)
CHUNK_STEP = (0, 3)
SUM_STEP, OUT_STEP = 5, 6
TPAIRS = TILES // 2
EPS = 1e-5


def build(nc, x_in, wq_in, wk_in, wv_in, wo_in, bo_in, wr_in, win_in, wout_in, bias_in, out):
    with ExitStack() as ctx:
        def sb(name, shape, dt=F32):
            return ctx.enter_context(nc.sbuf_tensor(name, shape, dt))

        def sem(name):
            return ctx.enter_context(nc.semaphore(name))

        bank = [ctx.enter_context(nc.psum_tensor(f"bank{i}", [P, 512], F32)) for i in range(8)]

        xn_dram = nc.dram_tensor("xn_scratch", (T, D), F32, kind="Internal").ap()
        y_dram = nc.dram_tensor("y_scratch", (TOPK * T + BLOCKS * P, D), F32, kind="Internal").ap()

        w_hi = sb("w_hi", [P, E, DK, 2 * H], F32R)
        w_lo = sb("w_lo", [P, E, DK, 2 * H], F32R)
        with ExitStack() as room:
            def room_sb(name, shape, dt=F32):
                return room.enter_context(nc.sbuf_tensor(name, shape, dt))

            wq, wk, wv, wo = [room_sb(name, [P, DK, D]) for name in ("wq", "wk", "wv", "wo")]
            v = room_sb("v", [P, TILES, HEADS, 3 * HD], BF16)
            v_rest = [room_sb(f"v_rest{u}", [P, HEADS, HD]) for u in range(2)]
            k_head = [room_sb(f"k_head{u}", [P, 2, 2, SEQ], F32R) for u in range(KSLOTS)]
        w_out = sb("w_out", [P, E, HK, D])
        ctxT = wv
        xT_hi = [sb(f"xT_hi{u}", [P, DK, P], F32R) for u in range(2)]
        xT_lo = [sb(f"xT_lo{u}", [P, DK, P], F32R) for u in range(2)]

        q_hi, q_lo = xT_hi, xT_lo

        with ExitStack() as room:
            pT_hi = [room_sb(f"pT_hi{u}", [P, 3, P], F16) for u in range(4)]
            pT_lo = [room_sb(f"pT_lo{u}", [P, 3, P], F16) for u in range(4)]
            ctxv = room_sb("ctxv", [P, 2, HEADS, HD])
            room_sb("xnT_place", [P, DK, T])
            probs = [room_sb(f"probs{u}", [P, 2, 3, P]) for u in range(2)]
            k_hi = room_sb("k_hi", [P, DK, SEQ], F32R)
            k_lo = room_sb("k_lo", [P, DK, SEQ], F32R)
        with ExitStack() as room:
            room_sb("block_place", [P, 2 * 2 * D + 2 * H])
            gT_hi = room_sb("gT_hi", [P, HK, P], F32R)
            gT_lo = room_sb("gT_lo", [P, HK, P], F32R)
            wo_hi = [room_sb(f"wo_hi{u}", [P, HK, D], F32R) for u in range(2)]
            wo_lo = room_sb("wo_lo", [P, HK, D], F32R)
        arena = sb("arena", [P, 2560 + TOPK * TILES * D])

        def view(base, at, shape, dt=F32, names="abc"):
            words = int(np.prod(shape)) // (1 if dt in (F32, F32R) else 2)
            v = base[:, at:at + words]
            if dt != F32:
                v = v.bitcast(dt)
            if len(shape) > 1:
                dims = names[:len(shape)]
                v = v.rearrange(f"p ({' '.join(dims)}) -> p {' '.join(dims)}", **dict(zip(dims[1:], shape[1:])))
            return v, at + words

        w_out_words = w_out[:, :, :, :].rearrange("p e c d -> p (e c d)")
        free_experts = E - 2 * STAGES
        stage = [view(w_out_words, (free_experts + 2 * i) * HK * D, [DK, 2 * H])[0] for i in range(STAGES)]
        xn, at = view(arena, 0, [TILES, D])
        xnT, at = view(arena, at, [DK, T])
        row_hot, at_hot = view(arena, at, [PAIRS, P], F16)
        blk_hot, at_hot = view(arena, at_hot, [PAIRS, BLOCKS])
        blk_pair, at_hot = view(arena, at_hot, [PAIRS, BLOCKS], F16)
        xb, y = [None] * 2, [None] * 2
        at = 0
        for i in range(2):
            xb[i], at = view(arena, at, [D])
            y[i], at = view(arena, at, [D])
        sa, at = view(arena, at, [H])
        g, at = view(arena, at, [H])
        y_in, at = view(arena, at + HK * P, [TOPK, TILES, D])

        wr = sb("wr", [P, DK, E])
        bias_half = sb("bias_half", [P, D])
        bo = sb("bo", [P, D])
        ident = sb("ident", [P, P])
        ident_b = sb("ident_b", [P, P], BF16)
        neg_mask = sb("neg_mask", [P, P], BF16)
        before = sb("before", [P, P], F16)
        ones = sb("ones", [P, P], F16)
        col = sb("col", [P, P])
        rev = sb("rev", [P, E])
        block_edge = sb("block_edge", [P, E])
        expert_before = sb("expert_before", [P, E, E])
        block_no = sb("block_no", [P, BLOCKS])
        pair_id = sb("pair_id", [P, PAIRS])
        trash_id = sb("trash_id", [P, BLOCKS])
        head_mask = sb("head_mask", [P, HPC])
        minus_half = sb("minus_half", [P, TILES])
        x = sb("x", [P, TILES, D])
        stats = sb("stats", [P, TILES, 6])
        mv = sb("mv", [P, TILES, 2])
        var_eps = sb("var_eps", [P, TILES])
        rstd = sb("rstd", [P, TILES])
        logits = sb("logits", [P, TILES, E])
        logits2 = sb("logits2", [P, TILES, E])
        top = sb("top", [P, TOPK, TILES])
        hit = sb("hit", [P, TILES, E])
        first = sb("first", [P, TILES])
        choice = sb("choice", [P, TOPK, TILES, E])
        chosen = sb("chosen", [P, TILES, E], F16)
        gap = sb("gap", [P, TILES])
        e1 = sb("e1", [P, TILES])
        den = sb("den", [P, TILES])
        gate = sb("gate", [P, TOPK, TILES])
        over_edge = sb("over_edge", [P, E, E])
        n_blocks = sb("n_blocks", [P, E])
        first_block = sb("first_block", [P, E])
        end_block = sb("end_block", [P, E])
        place = sb("place", [P, TILES, E])
        placed = sb("placed", [P, TOPK, TILES, E])
        slot = sb("slot", [P, PAIRS])
        slot_i = sb("slot_i", [P, PAIRS], I32)
        row_i = sb("row_i", [P, PAIRS], I32)
        blk_i = sb("blk_i", [P, PAIRS], I32)
        pair_of = sb("pair_of", [P, BLOCKS])
        empty = sb("empty", [P, BLOCKS])
        wrap = sb("wrap", [P, BLOCKS])
        scatter_row = sb("scatter_row", [P, BLOCKS], I32)
        gather_row = sb("gather_row", [P, BLOCKS], I32)
        past = sb("past", [P, BLOCKS, E])
        block_expert_f = sb("block_expert_f", [P, BLOCKS])
        block_expert = sb("block_expert", [P, BLOCKS], I32)
        neg_max = [sb(f"neg_max{u}", [P, 2, 2]) for u in range(2)]
        row_sum = placed[:, :, :, :].rearrange("p k i e -> p (k i e)")\
            .rearrange("p (b q h) -> p b q h", b=BATCH, q=2)
        inv_sum = sb("inv_sum", [P, 2, HEADS])

        x_loaded = [sem(f"x_loaded{i}") for i in range(TPAIRS)]
        small_loaded = sem("small_loaded")
        attn_w_loaded = sem("attn_w_loaded")
        stage_loaded = [sem(f"stage_loaded{i}") for i in range(STAGES)]
        w_hi_ready = sem("w_hi_ready")
        w_lo_front = sem("w_lo_front")
        w_lo_back = sem("w_lo_back")
        wout_loaded = sem("wout_loaded")
        xn_stored = sem("xn_stored")
        y_loaded = [sem(f"y_loaded{i}") for i in range(TPAIRS)]
        out_stored = sem("out_stored")
        const_step = sem("const_step")
        var_ready = sem("var_ready")
        rstd_ready = sem("rstd_ready")
        xn_ready = sem("xn_ready")
        xnT_in_psum = sem("xnT_in_psum")
        xnT_ready = sem("xnT_ready")
        bias_added = sem("bias_added")
        x_added = sem("x_added")
        logits_done = sem("logits_done")
        route_step = sem("route_step")
        chosen_ready = sem("chosen_ready")
        gap_ready = sem("gap_ready")
        e1_ready = sem("e1_ready")
        ranks_done = sem("ranks_done")
        hot_ready = sem("hot_ready")
        pairs_done = sem("pairs_done")
        plan_ready = sem("plan_ready")
        gathered = [sem(f"gathered{u}") for u in range(2)]
        xT_in_psum = sem("xT_in_psum")
        xT_hi_ready = sem("xT_hi_ready")
        xT_lo_ready = sem("xT_lo_ready")
        a_done = sem("a_done")
        b_done = sem("b_done")
        silu_done = sem("silu_done")
        g_done = sem("g_done")
        gT_in_psum = sem("gT_in_psum")
        gT_hi_ready = sem("gT_hi_ready")
        gT_lo_ready = sem("gT_lo_ready")
        wo_hi_ready = sem("wo_hi_ready")
        wo_lo_ready = sem("wo_lo_ready")
        y_done = sem("y_done")
        y_copied = sem("y_copied")
        scattered = [sem(f"scattered{u}") for u in range(2)]
        v_done = sem("v_done")
        v_first_ready = sem("v_first_ready")
        v_rest_ready = sem("v_rest_ready")
        v_second_ready = sem("v_second_ready")
        v_ready = sem("v_ready")
        qk_done = sem("qk_done")
        qk_hi_ready = sem("qk_hi_ready")
        qk_ready = sem("qk_ready")
        k_head_ready = sem("k_head_ready")
        tail_scored = sem("tail_scored")
        head_scored = sem("head_scored")
        tail_max_done = sem("tail_max_done")
        head_max_done = sem("head_max_done")
        head_probs_ready = sem("head_probs_ready")
        tail_probs_ready = sem("tail_probs_ready")
        probsT_done = sem("probsT_done")
        pT_hi_ready = sem("pT_hi_ready")
        pT_lo_ready = sem("pT_lo_ready")
        pv_done = sem("pv_done")
        inv_ready = sem("inv_ready")
        ctx_copied = sem("ctx_copied")
        ctx_summed = sem("ctx_summed")
        ctx_ready = sem("ctx_ready")
        ctxT_done = sem("ctxT_done")
        ctxT_ready = sem("ctxT_ready")
        o_done = sem("o_done")
        attn_added = sem("attn_added")

        block = ctx.enter_context(nc.Block())

        def after_first(f, j, n):
            return f or not isinstance(j, int) or j >= n

        def reach(eng, signal, count):
            if not isinstance(count, int) or count > 0:
                eng.wait_ge(signal, count)

        def sweep(eng, step):
            step(0, False, True)
            with eng.Fori(1, BATCH) as b:
                step(b, True, True)
            step(BATCH, True, False)

        def bc(ap, axis, shape):
            return ap.unsqueeze(axis).to_broadcast(shape)

        x_rows = x_in.rearrange("b (j p) d -> p (b j) d", p=P)
        out_rows = out.rearrange("b (j p) d -> p (b j) d", p=P)
        xn_rows = xn_dram.rearrange("(i p) d -> p i d", p=P)
        y_rows = y_dram[0:TOPK * T, :].rearrange("(k i p) d -> p k i d", p=P, k=TOPK)

        @block.sync
        def _(sp):
            for i in range(TPAIRS):
                rows = slice(2 * i, 2 * i + 2)
                sp.dma_start(x[:, rows, :], x_rows[:, rows, :]).then_inc(x_loaded[i], 16)
            sp.dma_start(wr[:, :, :], wr_in.rearrange("(k p) e -> p k e", p=P)).then_inc(small_loaded, 16)
            sp.dma_start(bias_half[:, :], bias_in.partition_broadcast(P)).then_inc(small_loaded, 16)
            sp.dma_start(bo[:, :], bo_in.partition_broadcast(P)).then_inc(small_loaded, 16)

            def load_w_out(first, last):
                sp.dma_start(w_out[:, first:last, :, :],
                             wout_in[first:last].rearrange("e (k p) n -> p (e k) n", p=P)).then_inc(wout_loaded, 16)

            def split(e):
                sp.wait_ge(w_hi_ready, e + 1)
                sp.wait_ge(w_lo_front, e + 1)
                sp.wait_ge(w_lo_back, e + 1)

            for e in range(E):
                if e >= STAGES:
                    split(e - STAGES)
                sp.dma_start(stage[e % STAGES][:, :, :], win_in[e].rearrange("(k p) n -> p k n", p=P))\
                    .then_inc(stage_loaded[e % STAGES], 16)
            load_w_out(0, free_experts)
            for e in range(E - STAGES, E):
                split(e)
                at = free_experts + 2 * (e % STAGES)
                load_w_out(at, at + 2)
            for f in range(2):
                if f == 0:
                    sp.wait_ge(y_done, BLOCKS)
                    for dst, src in ((wq, wq_in), (wk, wk_in), (wv, wv_in), (wo, wo_in)):
                        sp.dma_start(dst[:, :, :], src.rearrange("(k p) n -> p k n", p=P)).then_inc(attn_w_loaded, 16)
                else:
                    sp.wait_ge(o_done, BATCH)
                    for e in range(0, E, 2):
                        load_w_out(e, e + 2)
                sp.wait_ge(scattered[0], 16 * EVEN * (f + 1))
                sp.wait_ge(scattered[1], 16 * ODD * (f + 1))
                for i in range(TPAIRS):
                    for k in range(TOPK):
                        sp.dma_start(y_in[:, k, 2 * i:2 * i + 2, :], y_rows[:, k, 2 * i:2 * i + 2, :])\
                            .then_inc(y_loaded[i], 16)
            for i in range(0, TILES, 2):
                sp.wait_ge(x_added, TILES + i + 2)
                sp.dma_start(out_rows[:, i:i + 2, :], x[:, i:i + 2, :]).then_inc(out_stored, 16)
            sp.wait_ge(out_stored, 16 * TPAIRS)

        @block.gpsimd
        def _(pool):
            steps = [0]

            def then(ins):
                steps[0] += 1
                ins.then_inc(const_step, 1)
                pool.wait_ge(const_step, steps[0])

            def iota(t, pattern, base, mult):
                then(pool.iota(t, pattern, base=base, channel_multiplier=mult, allow_small_or_imprecise_dtypes=True))

            def select(t, pattern, base, mult, op, fill):
                then(pool.affine_select(out=t, in_=t, pattern=pattern, compare_op=op, fill=fill, base=base,
                                        channel_multiplier=mult))

            then(pool.memset(ident[:, :], 0.0))
            select(ident[:, :], [[-1, P]], 0, 1, ALU.not_equal, 1.0)
            then(pool.memset(minus_half[:, :], -0.5))
            iota(rev[:, :], [[-1, E]], E, 0)
            then(pool.memset(ones[:, :], 1.0))
            then(pool.memset(before[:, :], 1.0))
            select(before[:, :], [[1, P]], 0, -1, ALU.is_gt, 0.0)
            iota(block_edge[:, :], [[P, E]], 0, 0)
            then(pool.memset(expert_before[:, :, :], 1.0))
            select(expert_before[:, :, :], [[1, E], [-1, E]], 0, 0, ALU.is_gt, 0.0)
            iota(col[:, :], [[1, P]], 0, 0)
            iota(block_no[:, :], [[1, BLOCKS]], 0, 0)
            iota(pair_id[:, :].rearrange("p (k i) -> p k i", k=TOPK), [[T, TOPK], [P, TILES]], 1, 1)
            iota(trash_id[:, :], [[P, BLOCKS]], TOPK * T + 1, 1)
            then(pool.memset(neg_mask[:, :], 0.0))
            select(neg_mask[:, :], [[-1, P]], 0, 1, ALU.is_ge, NEG)
            then(pool.tensor_copy(ident_b[:, :], ident[:, :]))
            then(pool.memset(head_mask[:, :], 1.0))
            select(head_mask[:, :], [[-HD, HPC]], 0, 1, ALU.is_ge, 0.0)
            select(head_mask[:, :], [[HD, HPC]], HD - 1, -1, ALU.is_ge, 0.0)
            assert steps[0] == CONSTS
            pool.wait_ge(small_loaded, 48)
            then(pool.tensor_scalar(bias_half[:, :], bias_half[:, :], 0.5, None, ALU.mult))

            def inverse_root(phase):
                for i in range(TPAIRS):
                    pool.wait_ge(var_ready, TPAIRS * phase + i + 1)
                    two = slice(2 * i, 2 * i + 2)
                    pool.tensor_tensor(rstd[:, two], var_eps[:, two], minus_half[:, two], ALU.pow).then_inc(rstd_ready, 1)

            def split_back(e):
                pool.wait_ge(w_hi_ready, e + 1)
                pool.tensor_tensor(w_lo[:, e, 1, :], stage[e % STAGES][:, 1, :], w_hi[:, e, 1, :].bitcast(F32),
                                   ALU.subtract).then_inc(w_lo_back, 1)

            def add_bias(phase, b):
                pool.wait_ge(xn_ready, TILES * (phase + 1))
                pool.tensor_tensor(x[:, :, :], x[:, :, :], bc(b[:, :], 1, [P, TILES, D]), ALU.add)\
                    .then_inc(bias_added, 1)

            def gather(f, j):
                if f or j >= 2:
                    pool.wait_ge(xT_in_psum, f * BLOCKS + max(j - 1, 0))
                pool.indirect_dma_start(out=xb[j % 2][:, :], out_offset=None, in_=xn_dram,
                                        in_offset=bass.IndirectOffsetOnAxis(ap=gather_row[:, j:j + 1], axis=0))\
                    .then_inc(gathered[j % 2], 16)

            def scatter(f, j):
                pool.wait_ge(y_copied, f * BLOCKS + j + 1)
                pool.indirect_dma_start(out=y_dram, in_=y[j % 2][:, :], in_offset=None,
                                        out_offset=bass.IndirectOffsetOnAxis(ap=scatter_row[:, j:j + 1], axis=0))\
                    .then_inc(scattered[j % 2], 16)

            def ffn(f):
                inverse_root(2 * f)
                if f == 0:
                    for e in range(E):
                        split_back(e)
                pool.wait_ge(plan_ready, f + 1)
                pool.wait_ge(xn_stored, 16 * (f + 1))
                if f:
                    for i in range(TPAIRS):
                        pool.wait_ge(y_loaded[i], 16 * TOPK)
                for j in range(AHEAD):
                    gather(f, j)
                for j in range(BLOCKS):
                    if j + AHEAD < BLOCKS:
                        gather(f, j + AHEAD)
                    scatter(f, j)
                    if j == 2:
                        add_bias(2 * f, bias_half)

            ffn(0)
            inverse_root(1)
            add_bias(1, bo)

            def mask_keys(b, s):
                g = b * HPAIRS + (s - SLAG)
                p = (s - SLAG) % HPAIRS
                c = p // CPAIRS
                pool.wait_ge(qk_ready, (b * HPAIRS + (s - SLAG - p)) // HPAIRS * DK + c + 1 if isinstance(b, int)
                             else b * DK + (c + 1 - (DK if s < SLAG else 0)))
                reach(pool, head_scored, g + (1 - KSLOTS))
                for hh in range(2):
                    h = 2 * p + hh
                    for part, k in enumerate((k_hi, k_lo)):
                        ins = pool.tensor_tensor(k_head[s % KSLOTS][:, part, hh, :], k[:, c, :].bitcast(F32),
                                                 head_mask[:, h % HPC:h % HPC + 1].to_broadcast([P, SEQ]), ALU.mult)
                ins.then_inc(k_head_ready, 1)

            def step(b, old, new):
                for s in range(HPAIRS):
                    if old if s < SLAG else new:
                        mask_keys(b, s)
                    if s == SLAG and not old:
                        for t in range(TILES):
                            pool.wait_ge(v_second_ready, t + 1)
                            pool.tensor_tensor(v[:, t, :, 2 * HD:3 * HD], v_rest[t % 2][:, :, :], v[:, t, :, HD:2 * HD],
                                               ALU.subtract).then_inc(v_ready, 1)

            sweep(pool, step)
            ffn(1)

        @block.scalar
        def _(act):
            def turn_out(phase):
                for pair in range(TILES // 2):
                    act.wait_ge(xnT_in_psum, 4 * phase + pair + 1)
                    act.activation(xnT[:, :, pair * 256:(pair + 1) * 256],
                                   bank[pair % 2][:, :].rearrange("p (k t) -> p k t", k=DK), ACT.Copy)\
                        .then_inc(xnT_ready, 1)

            def split_front(e):
                act.wait_ge(stage_loaded[e % STAGES], 16 * (e // STAGES + 1))
                act.activation(w_hi[:, e, :, :], stage[e % STAGES][:, :, :], ACT.Copy).then_inc(w_hi_ready, 1)

            def copy_xT(f, j, u):
                act.wait_ge(xT_in_psum, f * BLOCKS + j + 1)
                if after_first(f, j, 2):
                    act.wait_ge(b_done, f * BLOCKS + j - 1)
                act.activation(xT_hi[u][:, :, :], bank[5][:, 0:D].rearrange("p (k t) -> p k t", k=DK), ACT.Copy)\
                    .then_inc(xT_hi_ready, 1)

            def silu(f, j, u):
                act.wait_ge(a_done, f * BLOCKS + j + 1)
                if after_first(f, j, 1):
                    act.wait_ge(g_done, f * BLOCKS + j)
                act.activation(sa[:, :], bank[u][:, :], ACT.Silu).then_inc(silu_done, 1)

            def copy_gT(f, j):
                act.wait_ge(gT_in_psum, f * BLOCKS + j + 1)
                if after_first(f, j, 1):
                    act.wait_ge(y_done, f * BLOCKS + j)
                act.activation(gT_hi[:, :, :], bank[4][:, :].rearrange("p (c t) -> p c t", c=HK), ACT.Copy)\
                    .then_inc(gT_hi_ready, 1)

            def split_out(f, j, u):
                e = act.value_load(block_expert[0:1, bass.ds(j, 1)], min_val=0, max_val=E - 1)
                if after_first(f, j, 2):
                    act.wait_ge(y_done, f * BLOCKS + j - 1)
                act.activation(wo_hi[u][:, :, :], w_out[:, bass.ds(e, 1), :, :].rearrange("p o c d -> p (o c) d"), ACT.Copy)\
                    .then_inc(wo_hi_ready, 1)

            def copy_y(f, j, u, scatters_before):
                act.wait_ge(y_done, f * BLOCKS + j + 1)
                if not isinstance(scatters_before, int) or scatters_before:
                    act.wait_ge(scattered[u], scatters_before * 16)
                act.activation(y[u][:, :], bank[6][:, 0:D], ACT.Copy).then_inc(y_copied, 1)

            def ffn(f):
                if f == 0:
                    split_front(0)
                turn_out(2 * f)
                act.wait_ge(xn_ready, TILES * (2 * f + 1))
                act.dma_start(xn_rows, xn[:, :, :]).then_inc(xn_stored, 16)
                if f == 0:
                    for e in range(1, E - 2):
                        split_front(e)
                act.wait_ge(gap_ready, f + 1)
                act.activation(e1[:, :], gap[:, :], ACT.Exp).then_inc(e1_ready, 1)
                if f == 0:
                    for e in range(E - 2, E):
                        split_front(e)
                base = (EVEN * f, ODD * f)
                copy_xT(f, 0, 0)
                silu(f, 0, 0)
                copy_xT(f, 1, 1)
                act.wait_ge(wout_loaded, 16 * (1 + STAGES) + 16 * f * E // 2)
                act.wait_ge(plan_ready, f + 1)
                split_out(f, 0, 0)

                def body(j, u, of_parity, silu_next=True, copy_next=True):
                    if silu_next:
                        silu(f, j + 1, 1 - u)
                    copy_gT(f, j)
                    if silu_next:
                        split_out(f, j + 1, 1 - u)
                    if copy_next:
                        copy_xT(f, j + 2, u)
                    copy_y(f, j, u, of_parity + base[u])

                for j in range(PEELED):
                    body(j, j % 2, j // 2)
                with act.Fori(0, LOOPED) as i:
                    for u in range(2):
                        body(i * 2 + (PEELED + u), (PEELED + u) % 2, i + (PEELED + u) // 2)
                for j in range(AFTER, BLOCKS):
                    body(j, j % 2, j // 2, j + 1 < BLOCKS, j + 2 < BLOCKS)

            ffn(0)
            turn_out(1)

            def chunk(b, c):
                act.wait_ge(qk_done, b * DK + (c + 1))
                reach(act, head_scored, b * HPAIRS + (CPAIRS * (c + 1) - HPAIRS))
                act.activation(q_hi[c][:, :, :], bank[7][:, 0:SEQ].rearrange("p (q t) -> p q t", q=2), ACT.Copy, scale=1.0 / SEQ ** 0.5)
                act.activation(k_hi[:, c, :], bank[7][:, SEQ:2 * SEQ], ACT.Copy).then_inc(qk_hi_ready, 1)

            def exps(b, s):
                g = b * HPAIRS + (s - SLAG)
                p, u = (s - SLAG) % HPAIRS, s % 2
                batch = b if s >= SLAG else b - 1
                act.wait_ge(tail_max_done, g + 1)
                reach(act, probsT_done, g * 2 - 2)
                for hh in range(2):
                    h = 2 * p + hh
                    act.activation(probs[u][:, hh, 1:3, :],
                                   bank[u][:, hh * SEQ:(hh + 1) * SEQ].rearrange("p (k t) -> p k t", k=2), ACT.Exp,
                                   bias=neg_max[u][:, 1, hh:hh + 1],
                                   accum_out=row_sum[:, bass.ds(batch, 1), 1, h:h + 1]).then_inc(tail_probs_ready, 1)
                act.wait_ge(head_max_done, g + 1)
                for hh in range(2):
                    h = 2 * p + hh
                    act.activation(probs[u][:, hh, 0, :], bank[2][:, P * hh:P * (hh + 1)], ACT.Exp,
                                   bias=neg_max[u][:, 0, hh:hh + 1],
                                   accum_out=row_sum[:, bass.ds(batch, 1), 0, h:h + 1]).then_inc(head_probs_ready, 1)

            def high(b, s):
                g = b * HPAIRS + (s - SLAG - 1)
                for hh in range(2):
                    act.wait_ge(probsT_done, g * 2 + (hh + 1))
                    reach(act, pv_done, g * 2 + (hh - 3))
                    act.activation(pT_hi[(s - 1) % 2 * 2 + hh][:, :, :],
                                   bank[3 + hh][:, 0:3 * P].rearrange("p (k t) -> p k t", k=3),
                                   ACT.Copy, scale=P_SCALE).then_inc(pT_hi_ready, 1)

            def step(b, old, new):
                for s in range(HPAIRS):
                    if new and s in CHUNK_STEP:
                        chunk(b, CHUNK_STEP.index(s))
                    if s == 1 and not old:
                        for t in range(TILES + 1):
                            if t < TILES:
                                act.wait_ge(v_done, t + 1)
                                act.activation(v[:, t, :, 0:HD],
                                               bank[VBANK[t % 4]][:, 0:D].rearrange("p (h d) -> p h d", h=HEADS),
                                               ACT.Copy).then_inc(v_first_ready, 1)
                            if t >= 1:
                                act.wait_ge(v_rest_ready, t)
                                act.activation(v[:, t - 1, :, HD:2 * HD], v_rest[(t - 1) % 2][:, :, :], ACT.Copy)\
                                    .then_inc(v_second_ready, 1)
                    if old and s == OUT_STEP:
                        act.wait_ge(ctxT_done, b)
                        act.activation(ctxT[:, :, :], bank[7][:, :].rearrange("p (k t) -> p k t", k=DK), ACT.Copy)\
                            .then_inc(ctxT_ready, 1)
                    if old if s < SLAG else new:
                        exps(b, s)
                    if old and s == SUM_STEP - 1:
                        act.wait_ge(pv_done, b * HEADS)
                        for qt in range(2):
                            cv = bank[5 + qt][:, :].rearrange("p (h w) -> p h w", w=2 * HD)
                            act.activation(ctxv[:, qt, :, :], cv[:, :, HD:2 * HD], ACT.Copy, scale=1.0 / P_SCALE)\
                                .then_inc(ctx_copied, 1)
                    if old if s < SLAG + 1 else new:
                        high(b, s)

            sweep(act, step)
            ffn(1)

        @block.vector
        def _(dve):
            steps = [0]

            def then(ins):
                steps[0] += 1
                ins.then_inc(route_step, 1)
                dve.wait_ge(route_step, steps[0])

            def measure(phase, i):
                two = slice(2 * i, 2 * i + 2)
                if phase == 0:
                    dve.wait_ge(x_loaded[i], 16)
                dve.bn_stats(stats[:, 2 * i, :], x[:, 2 * i, :])
                then(dve.bn_stats(stats[:, 2 * i + 1, :], x[:, 2 * i + 1, :]))
                dve.bn_aggr(mv[:, 2 * i, :], stats[:, 2 * i, :])
                then(dve.bn_aggr(mv[:, 2 * i + 1, :], stats[:, 2 * i + 1, :]))
                dve.tensor_scalar(var_eps[:, two], mv[:, two, 1], EPS, None, ALU.add).then_inc(var_ready, 1)

            def scale(phase, i):
                dve.wait_ge(rstd_ready, TPAIRS * phase + i + 1)
                for t in (2 * i, 2 * i + 1):
                    dve.tensor_scalar(xn[:, t, :], x[:, t, :], mv[:, t, 0:1], rstd[:, t:t + 1], ALU.subtract, ALU.mult)\
                        .then_inc(xn_ready, 1)

            def normalise(phase, before=None):
                for i in range(TPAIRS + 1):
                    if i < TPAIRS:
                        if before:
                            before(i)
                        measure(phase, i)
                    if i >= 1 and phase != 1:
                        scale(phase, i - 1)
                if phase == 1:
                    for i in range(TPAIRS):
                        scale(phase, i)

            def split_low(e):
                dve.wait_ge(w_hi_ready, e + 1)
                dve.tensor_tensor(w_lo[:, e, 0, :], stage[e % STAGES][:, 0, :], w_hi[:, e, 0, :].bitcast(F32),
                                  ALU.subtract).then_inc(w_lo_front, 1)

            def route(f):
                te = [P, TILES, E]
                if f == 0:
                    split_low(0)
                    split_low(1)
                dve.wait_ge(logits_done, f + 1)
                then(dve.tensor_copy(logits[:, :, :], bank[7][:, 0:TILES * E].rearrange("p (i e) -> p i e", e=E)))
                for k, values in enumerate((logits, logits2)):
                    then(dve.tensor_reduce(top[:, k, :], values[:, :, :], AX_X, ALU.max))
                    then(dve.tensor_tensor(hit[:, :, :], values[:, :, :], bc(top[:, k, :], 2, te), ALU.is_equal))
                    then(dve.tensor_tensor(hit[:, :, :], hit[:, :, :], bc(rev[:, :], 1, te), ALU.mult))
                    then(dve.tensor_reduce(first[:, :], hit[:, :, :], AX_X, ALU.max))
                    then(dve.tensor_tensor(choice[:, k, :, :], bc(rev[:, :], 1, te), bc(first[:, :], 2, te), ALU.is_equal))
                    if k == 0:
                        then(dve.scalar_tensor_tensor(logits2[:, :, :], choice[:, 0, :, :], -3.0e38, logits[:, :, :],
                                                      ALU.mult, ALU.add))
                dve.tensor_tensor(chosen[:, :, :], choice[:, 0, :, :], choice[:, 1, :, :], ALU.add).then_inc(chosen_ready, 1)
                dve.tensor_tensor(gap[:, :], top[:, 1, :], top[:, 0, :], ALU.subtract).then_inc(gap_ready, 1)
                if f == 0:
                    split_low(2)
                    split_low(3)
                dve.wait_ge(ranks_done, f + 1)
                then(dve.tensor_tensor(over_edge[:, :, :], bc(bank[6][:, 0:E], 2, [P, E, E]),
                                       bc(block_edge[:, :], 1, [P, E, E]), ALU.is_gt))
                then(dve.tensor_reduce(n_blocks[:, :], over_edge[:, :, :], AX_X, ALU.add))
                then(dve.tensor_tensor(over_edge[:, :, :], expert_before[:, :, :], bc(n_blocks[:, :], 1, [P, E, E]), ALU.mult))
                then(dve.tensor_reduce(first_block[:, :], over_edge[:, :, :], AX_X, ALU.add))
                then(dve.tensor_tensor(end_block[:, :], first_block[:, :], n_blocks[:, :], ALU.add))
                then(dve.scalar_tensor_tensor(place[:, :, :], bc(first_block[:, :], 1, te), float(P),
                                              bank[4][:, 0:TILES * E].rearrange("p (i e) -> p i e", e=E),
                                              ALU.mult, ALU.add))
                for k in range(TOPK):
                    then(dve.tensor_tensor(placed[:, k, :, :], choice[:, k, :, :], place[:, :, :], ALU.mult))
                then(dve.tensor_reduce(slot[:, :].rearrange("p (k i) -> p k i", k=TOPK), placed[:, :, :, :], AX_X, ALU.add))
                then(dve.tensor_copy(slot_i[:, :], slot[:, :]))
                then(dve.tensor_scalar(row_i[:, :], slot_i[:, :], P - 1, None, ALU.bitwise_and))
                then(dve.tensor_scalar(blk_i[:, :], slot_i[:, :], 7, None, ALU.logical_shift_right))
                then(dve.tensor_tensor(blk_hot[:, :, :], bc(blk_i[:, :], 2, [P, PAIRS, BLOCKS]),
                                       bc(block_no[:, :], 1, [P, PAIRS, BLOCKS]), ALU.is_equal))
                then(dve.tensor_tensor(blk_pair[:, :, :], blk_hot[:, :, :], bc(pair_id[:, :], 2, [P, PAIRS, BLOCKS]), ALU.mult))
                dve.tensor_tensor(row_hot[:, :, :], bc(row_i[:, :], 2, [P, PAIRS, P]), bc(col[:, :], 1, [P, PAIRS, P]),
                                  ALU.is_equal).then_inc(hot_ready, 1)
                then(dve.tensor_tensor(past[:, :, :], bc(end_block[:, :], 1, [P, BLOCKS, E]),
                                       bc(block_no[:, :], 2, [P, BLOCKS, E]), ALU.is_le))
                then(dve.tensor_reduce(block_expert_f[:, :], past[:, :, :], AX_X, ALU.add))
                then(dve.tensor_scalar(block_expert[:, :], block_expert_f[:, :], float(E - 1), None, ALU.min))
                if f == 0:
                    split_low(4)
                    split_low(5)
                dve.wait_ge(pairs_done, f + 1)
                then(dve.tensor_copy(pair_of[:, :], bank[7][:, 0:BLOCKS]))
                then(dve.scalar_tensor_tensor(empty[:, :], pair_of[:, :], 0.0, trash_id[:, :], ALU.is_equal, ALU.mult))
                then(dve.scalar_tensor_tensor(scatter_row[:, :], pair_of[:, :], 1.0, empty[:, :], ALU.subtract, ALU.add))
                then(dve.tensor_scalar(wrap[:, :], pair_of[:, :], T + 0.5, -float(T), ALU.is_gt, ALU.mult))
                then(dve.scalar_tensor_tensor(wrap[:, :], pair_of[:, :], 1.0, wrap[:, :], ALU.subtract, ALU.add))
                dve.tensor_scalar(gather_row[:, :], wrap[:, :], 0.0, None, ALU.max).then_inc(plan_ready, 1)
                if f == 0:
                    split_low(6)
                    split_low(7)
                dve.wait_ge(e1_ready, f + 1)
                then(dve.tensor_scalar(den[:, :], e1[:, :], 1.0, None, ALU.add))
                then(dve.reciprocal(den[:, :], den[:, :]))
                then(dve.tensor_scalar(gate[:, 0, :], den[:, :], 0.5, None, ALU.mult))
                then(dve.tensor_tensor(gate[:, 1, :], gate[:, 0, :], e1[:, :], ALU.mult))

            def copy_xT_low(f, j, u):
                dve.wait_ge(xT_hi_ready, f * BLOCKS + j + 1)
                if after_first(f, j, 2):
                    dve.wait_ge(b_done, f * BLOCKS + j - 1)
                dve.tensor_tensor(xT_lo[u][:, :, :], bank[5][:, 0:D].rearrange("p (k t) -> p k t", k=DK),
                                  xT_hi[u][:, :, :].bitcast(F32), ALU.subtract).then_inc(xT_lo_ready, 1)

            def expert(j):
                return dve.value_load(block_expert[0:1, bass.ds(j, 1)], min_val=0, max_val=E - 1)

            def split_out_low(f, j, u, e):
                dve.wait_ge(wo_hi_ready, f * BLOCKS + j + 1)
                if after_first(f, j, 1):
                    dve.wait_ge(y_done, f * BLOCKS + j)
                dve.tensor_tensor(wo_lo[:, :, :], w_out[:, bass.ds(e, 1), :, :].rearrange("p o c d -> p (o c) d"),
                                  wo_hi[u][:, :, :].bitcast(F32), ALU.subtract).then_inc(wo_lo_ready, 1)

            def copy_gT_low(f, j):
                dve.wait_ge(gT_hi_ready, f * BLOCKS + j + 1)
                dve.tensor_tensor(gT_lo[:, :, :], bank[4][:, :].rearrange("p (c t) -> p c t", c=HK),
                                  gT_hi[:, :, :].bitcast(F32), ALU.subtract).then_inc(gT_lo_ready, 1)

            def gated(f, j, u):
                dve.wait_ge(b_done, f * BLOCKS + j + 1)
                dve.wait_ge(silu_done, f * BLOCKS + j + 1)
                if after_first(f, j, 1):
                    dve.wait_ge(gT_in_psum, f * BLOCKS + j)
                dve.tensor_tensor(g[:, :], sa[:, :], bank[2 + u][:, :], ALU.mult).then_inc(g_done, 1)

            def add_rows(f, i):
                dve.wait_ge(y_loaded[i], 16 * TOPK * (f + 1))
                for k in range(TOPK):
                    for t in (2 * i, 2 * i + 1):
                        ins = dve.scalar_tensor_tensor(x[:, t, :], y_in[:, k, t, :], gate[:, k, t:t + 1], x[:, t, :],
                                                       ALU.mult, ALU.add)
                        if k == TOPK - 1:
                            ins.then_inc(x_added, 1)
                    if k == 0:
                        then(ins)
                dve.wait_ge(x_added, TILES * f + 2 * i + 2)

            def ffn(f):
                route(f)
                copy_xT_low(f, 0, 0)
                copy_xT_low(f, 1, 1)
                first = expert(0)
                gated(f, 0, 0)
                split_out_low(f, 0, 0, first)

                def body(j, u, gate_next=True, copy_next=True):
                    if gate_next:
                        e = expert(j + 1)
                    copy_gT_low(f, j)
                    if copy_next:
                        copy_xT_low(f, j + 2, u)
                    if gate_next:
                        gated(f, j + 1, 1 - u)
                        split_out_low(f, j + 1, 1 - u, e)

                for j in range(PEELED):
                    body(j, j % 2)
                with dve.Fori(0, LOOPED) as i:
                    for u in range(2):
                        body(i * 2 + (PEELED + u), (PEELED + u) % 2)
                for j in range(AFTER, BLOCKS):
                    body(j, j % 2, j + 1 < BLOCKS, j + 2 < BLOCKS)
                dve.wait_ge(bias_added, 2 * f + 1)

            normalise(0)
            ffn(0)
            normalise(1, before=lambda i: add_rows(0, i))
            dve.wait_ge(bias_added, 2)

            def chunk(b, c):
                dve.wait_ge(qk_hi_ready, b * DK + (c + 1))
                dve.scalar_tensor_tensor(q_lo[c][:, :, :], bank[7][:, 0:SEQ].rearrange("p (q t) -> p q t", q=2),
                                         1.0 / SEQ ** 0.5, q_hi[c][:, :, :].bitcast(F32),
                                         ALU.mult, ALU.subtract)
                dve.tensor_tensor(k_lo[:, c, :], bank[7][:, SEQ:2 * SEQ], k_hi[:, c, :].bitcast(F32), ALU.subtract)\
                    .then_inc(qk_ready, 1)

            def maxima(b, s, tail):
                g = b * HPAIRS + (s - SLAG)
                u = s % 2
                if tail:
                    dve.wait_ge(tail_scored, g + 1)
                    reach(dve, tail_probs_ready, g * 2 - 2)
                    dve.tensor_reduce(neg_max[u][:, 1, :], bank[u][:, :].rearrange("p (h k) -> p h k", h=2),
                                      AX_X, ALU.max, negate=True).then_inc(tail_max_done, 1)
                else:
                    dve.wait_ge(head_scored, g + 1)
                    dve.tensor_reduce(neg_max[u][:, 0, :], bank[2][:, 0:2 * P].rearrange("p (h k) -> p h k", h=2),
                                      AX_X, ALU.max, negate=True).then_inc(head_max_done, 1)

            def low(b, s):
                g = b * HPAIRS + (s - SLAG - 2)
                for hh in range(2):
                    u = s % 2 * 2 + hh
                    dve.wait_ge(pT_hi_ready, g * 2 + (hh + 1))
                    dve.scalar_tensor_tensor(pT_lo[u][:, :, :], bank[3 + hh][:, 0:3 * P].rearrange("p (k t) -> p k t", k=3),
                                             P_SCALE, pT_hi[u][:, :, :], ALU.mult, ALU.subtract).then_inc(pT_lo_ready, 1)

            def add_up(b):
                sums = row_sum[:, bass.ds(b - 1, 1), :, :].rearrange("p o q h -> p (o q) h")
                dve.wait_ge(pv_done, b * HEADS)
                dve.reciprocal(inv_sum[:, :, :], sums).then_inc(inv_ready, 1)
                for qt in range(2):
                    cv = bank[5 + qt][:, :].rearrange("p (h w) -> p h w", w=2 * HD)
                    dve.wait_ge(ctx_copied, b * 2 + (qt - 1))
                    dve.scalar_tensor_tensor(ctxv[:, qt, :, :], cv[:, :, 0:HD], 1.0 / P_SCALE, ctxv[:, qt, :, :],
                                             ALU.mult, ALU.add).then_inc(ctx_summed, 1)

            def divide(b):
                dve.wait_ge(inv_ready, b)
                dve.wait_ge(ctx_summed, b * 2)
                for qt in range(2):
                    ins = dve.tensor_tensor(ctxv[:, qt, :, :], ctxv[:, qt, :, :],
                                            bc(inv_sum[:, qt, :], 2, [P, HEADS, HD]), ALU.mult)
                ins.then_inc(ctx_ready, 1)

            def add_attention(b):
                dve.wait_ge(o_done, b)
                rows = x[:, bass.ds(b * 2 - 2, 2), :]
                dve.tensor_tensor(rows, rows, bank[7][:, :].rearrange("p (q d) -> p q d", q=2), ALU.add)\
                    .then_inc(attn_added, 1)

            def step(b, old, new):
                for s in range(HPAIRS):
                    if s == 1 and not old:
                        for t in range(TILES):
                            dve.wait_ge(v_first_ready, t + 1)
                            reach(dve, v_ready, t - 1)
                            dve.tensor_tensor(v_rest[t % 2][:, :, :],
                                              bank[VBANK[t % 4]][:, 0:D].rearrange("p (h d) -> p h d", h=HEADS),
                                              v[:, t, :, 0:HD], ALU.subtract).then_inc(v_rest_ready, 1)
                    if old and s == SUM_STEP:
                        add_up(b)
                    if old and s == OUT_STEP + 1:
                        add_attention(b)
                    if old if s < SLAG else new:
                        maxima(b, s, True)
                    if new and s in CHUNK_STEP:
                        chunk(b, CHUNK_STEP.index(s))
                    if old if s < SLAG else new:
                        maxima(b, s, False)
                    if old and s == SUM_STEP:
                        divide(b)
                    if old if s < SLAG + 2 else new:
                        low(b, s)

            sweep(dve, step)
            dve.wait_ge(attn_added, BATCH)
            normalise(2)
            ffn(1)
            for i in range(TPAIRS):
                add_rows(1, i)

        @block.tensor
        def _(pe):
            def turn(phase):
                for pair in range(TILES // 2):
                    pe.wait_ge(xn_ready, TILES * phase + 2 * pair + 2)
                    if pair >= 2:
                        pe.wait_ge(xnT_ready, 4 * phase + pair - 1)
                    for k in range(DK):
                        for i in range(2):
                            at = k * 256 + i * P
                            last = pe.transpose(bank[pair % 2][:, at:at + P], xn[:, 2 * pair + i, k * P:(k + 1) * P],
                                                ident[:, :])
                    last.then_inc(xnT_in_psum, 1)

            def route(f):
                for i in range(TILES):
                    if i % 2 == 0:
                        pe.wait_ge(xnT_ready, 8 * f + i // 2 + 1)
                    for k in range(DK):
                        last = pe.matmul(bank[7][:, i * E:(i + 1) * E], xnT[:, k, i * P:(i + 1) * P], wr[:, k, :],
                                         start=(k == 0), stop=(k == DK - 1))
                last.then_inc(logits_done, 1)
                pe.wait_ge(chosen_ready, f + 1)
                flat = chosen[:, :, :].rearrange("p i e -> p (i e)")
                pe.matmul(bank[4][:, 0:TILES * E], before[:, :], flat, start=True, stop=False, skip_group_check=True)
                for i in range(TILES - 1):
                    left = TILES - 1 - i
                    pe.matmul(bank[4][:, (i + 1) * E:TILES * E].rearrange("p (i e) -> p i e", e=E), ones[:, :],
                              bc(chosen[:, i, :], 1, [P, left, E]), start=False, stop=(left == 1), skip_group_check=True)
                for i in range(TILES):
                    last = pe.matmul(bank[6][:, 0:E], ones[:, :], chosen[:, i, :], start=(i == 0), stop=(i == TILES - 1))
                last.then_inc(ranks_done, 1)
                pe.wait_ge(hot_ready, f + 1)
                for q in range(PAIRS):
                    last = pe.matmul(bank[7][:, 0:BLOCKS], row_hot[:, q, :], blk_pair[:, q, :], start=(q == 0),
                                     stop=(q == PAIRS - 1))
                last.then_inc(pairs_done, 1)

            def turn_block(f, j, u, gathers):
                pe.wait_ge(gathered[u], gathers * 16)
                if after_first(f, j, 1):
                    pe.wait_ge(xT_lo_ready, f * BLOCKS + j)
                for k in range(DK):
                    last = pe.transpose(bank[5][:, k * P:(k + 1) * P], xb[u][:, k * P:(k + 1) * P], ident[:, :])
                last.then_inc(xT_in_psum, 1)

            def expert(j):
                return pe.value_load(block_expert[0:1, bass.ds(j, 1)], min_val=0, max_val=E - 1)

            def project(f, j, u, half, e):
                if half == 0:
                    pe.wait_ge(xT_hi_ready, f * BLOCKS + j + 1)
                    if f == 0:
                        pe.wait_ge(w_lo_front, e + 1)
                        pe.wait_ge(w_lo_back, e + 1)
                    if after_first(f, j, 2):
                        pe.wait_ge(silu_done, f * BLOCKS + j - 1)
                elif after_first(f, j, 2):
                    pe.wait_ge(g_done, f * BLOCKS + j - 1)
                for part, (tok, wts) in enumerate(((xT_hi, w_hi), (xT_hi, w_lo), (xT_lo, w_hi))):
                    if half == 0 and part == 2:
                        pe.wait_ge(xT_lo_ready, f * BLOCKS + j + 1)
                    for k in range(DK):
                        last = pe.matmul(bank[2 * half + u][:, :], tok[u][:, k, :],
                                         wts[:, bass.ds(e, 1), k, half * H:(half + 1) * H],
                                         start=(part == 0 and k == 0), stop=(part == 2 and k == DK - 1))
                last.then_inc(b_done if half else a_done, 1)

            def turn_gated(f, j, u):
                pe.wait_ge(g_done, f * BLOCKS + j + 1)
                if after_first(f, j, 1):
                    pe.wait_ge(gT_lo_ready, f * BLOCKS + j)
                for c in range(HK):
                    last = pe.transpose(bank[4][:, c * P:(c + 1) * P], g[:, c * P:(c + 1) * P], ident[:, :])
                last.then_inc(gT_in_psum, 1)

            def combine(f, j, u):
                pe.wait_ge(gT_hi_ready, f * BLOCKS + j + 1)
                if after_first(f, j, 1):
                    pe.wait_ge(y_copied, f * BLOCKS + j)
                for part, (tok, wts, ready) in enumerate(((gT_hi, wo_hi[u], wo_hi_ready), (gT_hi, wo_lo, wo_lo_ready),
                                                          (gT_lo, wo_hi[u], gT_lo_ready))):
                    pe.wait_ge(ready, f * BLOCKS + j + 1)
                    for c in range(HK):
                        last = pe.matmul(bank[6][:, 0:D], tok[:, c, :], wts[:, c, :], start=(part == 0 and c == 0),
                                         stop=(part == 2 and c == HK - 1))
                last.then_inc(y_done, 1)

            def ffn(f):
                turn(2 * f)
                if f == 0:
                    pe.wait_ge(small_loaded, 48)
                route(f)
                pe.wait_ge(plan_ready, f + 1)
                base = (EVEN * f, ODD * f)
                turn_block(f, 0, 0, base[0] + 1)
                first = expert(0)
                project(f, 0, 0, 0, first)
                project(f, 0, 0, 1, first)
                second = expert(1)
                turn_block(f, 1, 1, base[1] + 1)
                project(f, 1, 1, 0, second)
                turn_gated(f, 0, 0)
                project(f, 1, 1, 1, second)

                def body(j, u, of_parity, gated_next=True, block_next=True):
                    if block_next:
                        e = expert(j + 2)
                        turn_block(f, j + 2, u, of_parity + (base[u] + 2))
                    combine(f, j, u)
                    if block_next:
                        project(f, j + 2, u, 0, e)
                    if gated_next:
                        turn_gated(f, j + 1, 1 - u)
                    if block_next:
                        project(f, j + 2, u, 1, e)

                for j in range(PEELED):
                    body(j, j % 2, j // 2)
                with pe.Fori(0, LOOPED) as i:
                    for u in range(2):
                        body(i * 2 + (PEELED + u), (PEELED + u) % 2, i + (PEELED + u) // 2)
                for j in range(AFTER, BLOCKS):
                    body(j, j % 2, j // 2, j + 1 < BLOCKS, j + 2 < BLOCKS)

            pe.wait_ge(const_step, CONSTS)
            ffn(0)
            turn(1)
            pe.wait_ge(attn_w_loaded, 64)
            pe.wait_ge(xnT_ready, 8)

            def chunk(b, c):
                reach(pe, qk_ready, b * DK + c)
                for w, to in ((wq, 0), (wk, SEQ)):
                    for k in range(DK):
                        last = pe.matmul(bank[7][:, to:to + SEQ], w[:, k, c * P:(c + 1) * P], xnT[:, k, bass.ds(b * SEQ, SEQ)],
                                         start=(k == 0), stop=(k == DK - 1))
                last.then_inc(qk_done, 1)

            def values():
                for t in range(TILES):
                    reach(pe, v_rest_ready, t - 3)
                    for k in range(DK):
                        last = pe.matmul(bank[VBANK[t % 4]][:, 0:D], xnT[:, k, t * P:(t + 1) * P], wv[:, k, :],
                                         start=(k == 0), stop=(k == DK - 1))
                    last.then_inc(v_done, 1)
                pe.wait_ge(v_rest_ready, TILES)

            def scores(b, s, tail):
                g = b * HPAIRS + (s - SLAG)
                c, u = (s - SLAG) % HPAIRS // CPAIRS, s % 2
                keys = k_head[s % KSLOTS]
                mask = bc(neg_mask[:, :], 1, [P, 2, P])
                if tail:
                    pe.wait_ge(k_head_ready, g + 1)
                    reach(pe, tail_probs_ready, g * 2 - 2)
                    to = bank[u][:, :].rearrange("p (h k) -> p h k", h=2)
                else:
                    reach(pe, head_probs_ready, g * 2)
                    to = bank[2][:, 0:2 * P].rearrange("p (h k) -> p h k", h=2)
                width = SEQ if tail else P
                for n, (q, part) in enumerate(((q_hi[c], 0), (q_hi[c], 1), (q_lo[c], 0))):
                    pe.matmul(to, q[:, 1 if tail else 0, :], keys[:, part, :, 0:width], start=(n == 0), stop=False)
                pe.matmul(to[:, :, width - P:width], ident_b[:, :], mask, start=False, stop=True)\
                    .then_inc(tail_scored if tail else head_scored, 1)

            def turn_probs(b, s):
                g = b * HPAIRS + (s - SLAG - 2)
                for hh in range(2):
                    pe.wait_ge(head_probs_ready, g * 2 + (hh + 1))
                    reach(pe, pT_lo_ready, g * 2 + (hh - 1))
                    for i in range(3):
                        last = pe.transpose(bank[3 + hh][:, i * P:(i + 1) * P], probs[s % 2][:, hh, i, :], ident[:, :])
                    last.then_inc(probsT_done, 1)

            def weigh(b, s):
                g = b * HPAIRS + (s - SLAG - 3)
                ago = s < SLAG + 3
                for hh in range(2):
                    h = 2 * ((s - SLAG - 3) % HPAIRS) + hh
                    u = (s - 1) % 2 * 2 + hh
                    pe.wait_ge(pT_lo_ready, g * 2 + (hh + 1))
                    both, second = slice(2 * HD * h, 2 * HD * (h + 1)), slice(2 * HD * h + HD, 2 * HD * (h + 1))
                    for i, (qt, kt) in enumerate(((0, 0), (1, 0), (1, 1))):
                        rows = v[:, bass.ds(b * 2 + (kt - 2 * ago), 1), h, :]
                        to = bank[5 + qt]
                        pe.matmul(to[:, both], pT_hi[u][:, i, :], rows[:, :, 0:2 * HD], start=(kt == 0), stop=False)
                        pe.matmul(to[:, second], pT_hi[u][:, i, :], rows[:, :, 2 * HD:3 * HD], start=False, stop=False)
                        last = pe.matmul(to[:, both], pT_lo[u][:, i, :], rows[:, :, 0:2 * HD], start=False, stop=(kt == qt))
                    last.then_inc(pv_done, 1)

            def turn_context(b, new):
                pe.wait_ge(ctx_ready, b)
                if new:
                    pe.wait_ge(qk_ready, b * DK + DK)
                for c in range(DK):
                    for qt in range(2):
                        heads = ctxv[:, qt, c * HPC:(c + 1) * HPC, :].rearrange("p h d -> p (h d)")
                        last = pe.transpose(bank[7][:, c * SEQ + qt * P:c * SEQ + (qt + 1) * P], heads, ident[:, :])
                last.then_inc(ctxT_done, 1)

            def project_out(b):
                pe.wait_ge(ctxT_ready, b)
                for qt in range(2):
                    for c in range(DK):
                        last = pe.matmul(bank[7][:, qt * D:(qt + 1) * D], ctxT[:, c, qt * P:(qt + 1) * P], wo[:, c, :],
                                         start=(c == 0), stop=(c == DK - 1))
                last.then_inc(o_done, 1)

            def step(b, old, new):
                for s in range(HPAIRS):
                    if s == 1 and not old:
                        values()
                    if old and s == OUT_STEP:
                        turn_context(b, new)
                    if old if s < SLAG else new:
                        scores(b, s, True)
                    if old if s < SLAG + 2 else new:
                        turn_probs(b, s)
                    if new and s in CHUNK_STEP:
                        chunk(b, CHUNK_STEP.index(s))
                    if old if s < SLAG else new:
                        scores(b, s, False)
                    if old if s < SLAG + 3 else new:
                        if s == SLAG + 3:
                            pe.wait_ge(*((ctx_summed, b * 2) if old else (v_ready, TILES)))
                        weigh(b, s)
                    if old and s == OUT_STEP:
                        project_out(b)
                if old and new:
                    pe.wait_ge(attn_added, b)

            sweep(pe, step)
            ffn(1)


def kernel(**inputs):
    import concourse.bacc as bacc
    from concourse.bass_utils import run_bass_kernel_spmd

    def lay(name, turned=False):
        a = np.asarray(inputs[name])
        return np.ascontiguousarray(np.swapaxes(a, -1, -2) if turned else a)

    arrays = {
        "x": lay("L0_attn_inputs"),
        "wq_t": lay("L0_attn_w_q", True),
        "wk_t": lay("L0_attn_w_k", True),
        "wv_t": lay("L0_attn_w_v", True),
        "wo_t": lay("L0_attn_w_o", True),
        "bo": lay("L0_attn_b_o"),
        "wr_t": lay("L0_ffn_router_weight", True),
        "win_t": lay("L0_ffn_w_in", True),
        "wout_t": lay("L0_ffn_w_out", True),
        "bias": lay("L0_ffn_bias"),
    }
    nc = bacc.Bacc("TRN2", target_bir_lowering=False, num_devices=1)
    ins = [nc.dram_tensor(f"in_{n}", a.shape, F32, kind="ExternalInput").ap() for n, a in arrays.items()]
    out = nc.dram_tensor("out", (BATCH, SEQ, D), F32, kind="ExternalOutput").ap()
    build(nc, *ins, out)
    return run_bass_kernel_spmd(nc, [{f"in_{n}": a for n, a in arrays.items()}], core_ids=[0]).results[0]["out"]
```

```python
from contextlib import ExitStack

import numpy as np

import concourse.bass as bass
from concourse import mybir

ALU = mybir.AluOpType
ACT = mybir.ActivationFunctionType
F32 = mybir.dt.float32
F16 = mybir.dt.float16
BF16 = mybir.dt.bfloat16
I32 = mybir.dt.int32
U32 = mybir.dt.uint32
F32R = mybir.dt.float32r
AX_X = mybir.AxisListType.X

P = 128
BATCH, SEQ, D = 4, 256, 256
T = BATCH * SEQ
TILES = T // P
DK = D // P
E, TOPK, H = 8, 2, 512
HK = H // P
HEADS, HD = 16, 16
HPC = P // HD
HPAIRS = HEADS // 2
CPAIRS = HPC // 2
SLAG = 2
BLOCKS = (TOPK * T + E * (P - 1)) // P
EVEN, ODD = (BLOCKS + 1) // 2, BLOCKS // 2
LAST = 2
SCATTERED = BLOCKS - LAST
S_EVEN, S_ODD = (SCATTERED + 1) // 2, SCATTERED // 2
ACC_BANK = (7, 5, 3, 2)
PE_ROWS = (((1, 1), (2, 1), (3, 1), (3, 0)), ((1, 1), (2, 1), (3, 1)))
DVE_ROWS = tuple(tuple((i, k) for i in range(T // P // 2) for k in range(TOPK) if (i, k) not in rows) for rows in PE_ROWS)
PAIRS = TOPK * TILES
NEG = -1.0e30
AHEAD = 4
TURN_AFTER = 5
FULL = TOPK * T // P
PEELED = 3
LOOPED = (BLOCKS - 2 - PEELED) // 2
AFTER = PEELED + 2 * LOOPED
STAGES = 3
CONSTS = 20
IDENT_CONSTS = 3
KSLOTS = 2
P_SCALE = 2.0 ** 15
VBANK = (6, 4, 5, 3, 5, 6, 5, 6)
VALUES = {1: (0, 2), 2: (2, 4), 3: (4, 6), 4: (6, 8)}
THIRDS = {2: (0, 2), 3: (2, 4), 4: (4, 6), 5: (6, 8)}
VSLOTS = 4
LBANK = (3, 2)
CHUNK_STEP = (0, 3)
SUM_STEP, OUT_STEP = 5, 6
POOL_LEAD = 1
BIAS_STEP = 4
WARM_START, WARM_RANKS, WARM_PLAN, WARM_TURNED = 12, (0, 18), (8, 6), (0, 4)
WARM_END, WARM_CONTEXT, WARM_SCORES, WARM_LAST = 2, 4, 7, 3
WARM_TURN = (5, 3)
TPAIRS = TILES // 2
EPS = 1e-5


def build(nc, x_in, wq_in, wk_in, wv_in, wo_in, bo_in, wr_in, win_in, wout_in, bias_in, out):
    with ExitStack() as ctx:
        def sb(name, shape, dt=F32):
            return ctx.enter_context(nc.sbuf_tensor(name, shape, dt))

        def sem(name):
            return ctx.enter_context(nc.semaphore(name))

        bank = [ctx.enter_context(nc.psum_tensor(f"bank{i}", [P, 512], F32)) for i in range(8)]

        gate_dram = nc.dram_tensor("gate_scratch", (TOPK * T, 1), F32, kind="Internal").ap()
        xn_dram = nc.dram_tensor("xn_scratch", (T, D), F32, kind="Internal").ap()
        y_dram = nc.dram_tensor("y_scratch", (TOPK * T + BLOCKS * P, D), F32, kind="Internal").ap()

        w_hi = sb("w_hi", [P, E, DK, 2 * H], F32R)
        w_lo = sb("w_lo", [P, E, DK, 2 * H], F32R)
        with ExitStack() as room:
            slot_hot = [room.enter_context(nc.sbuf_tensor(f"slot_hot{k}", [P, TILES, P], F32R)) for k in range(LAST)]
        with ExitStack() as room:
            def room_sb(name, shape, dt=F32):
                return room.enter_context(nc.sbuf_tensor(name, shape, dt))

            v = room_sb("v", [P, TILES, HEADS, 3 * HD], BF16)
            v_rest = [room_sb(f"v_rest{u}", [P, HEADS, HD]) for u in range(VSLOTS)]
            with ExitStack() as inner_room:
                k_head = [inner_room.enter_context(nc.sbuf_tensor(f"k_head{u}", [P, 2, 2, SEQ], F32R)) for u in range(KSLOTS)]
            xnT_late = room_sb("xnT_late", [P, DK, T])
            wq, wk, wv, wo = [room_sb(name, [P, DK, D]) for name in ("wq", "wk", "wv", "wo")]
        w_out = sb("w_out", [P, E, HK, D])
        ctxT = wv
        xT_hi = [sb(f"xT_hi{u}", [P, DK, P], F32R) for u in range(2)]
        xT_lo = [sb(f"xT_lo{u}", [P, DK, P], F32R) for u in range(2)]

        q_hi, q_lo = xT_hi, xT_lo

        with ExitStack() as room:
            pT_hi = [room_sb(f"pT_hi{u}", [P, 3, P], F16) for u in range(4)]
            pT_lo = [room_sb(f"pT_lo{u}", [P, 3, P], F16) for u in range(4)]
            ctxv = room_sb("ctxv", [P, 2, HEADS, HD])
            room_sb("xnT_place", [P, DK, T])
            probs = [room_sb(f"probs{u}", [P, 2, 3, P]) for u in range(2)]
            k_hi = room_sb("k_hi", [P, DK, SEQ], F32R)
            k_lo = room_sb("k_lo", [P, DK, SEQ], F32R)
        with ExitStack() as room:
            room_sb("block_place", [P, 2 * 2 * D + 2 * H])
            gT_hi = room_sb("gT_hi", [P, HK, P], F32R)
            gT_lo = room_sb("gT_lo", [P, HK, P], F32R)
            wo_hi = [room_sb(f"wo_hi{u}", [P, HK, D], F32R) for u in range(2)]
            wo_lo = room_sb("wo_lo", [P, HK, D], F32R)
            gated_last = [room_sb(f"gated_last{part}", [P, D], F32R) for part in range(2)]
        with ExitStack() as room:
            gated_before = [room_sb("gated_before0", [P, D], F32R), room_sb("y_place", [P, D]),
                            room_sb("gated_before1", [P, D], F32R)]
        gated_rows = [gated_before[0::2], gated_last]
        arena = sb("arena", [P, 2 * 2 * D + 2 * H + 2 * HK * P + 3 * HK * D + 2 * D])

        def view(base, at, shape, dt=F32, names="abc"):
            words = int(np.prod(shape)) // (1 if dt in (F32, F32R) else 2)
            v = base[:, at:at + words]
            if dt != F32:
                v = v.bitcast(dt)
            if len(shape) > 1:
                dims = names[:len(shape)]
                v = v.rearrange(f"p ({' '.join(dims)}) -> p {' '.join(dims)}", **dict(zip(dims[1:], shape[1:])))
            return v, at + words

        w_out_words = w_out[:, :, :, :].rearrange("p e c d -> p (e c d)")
        free_experts = E - 2 * STAGES
        stage_room = [free_experts + 2 * ((i - E) % STAGES) for i in range(STAGES)]
        stage = [view(w_out_words, room_at * HK * D, [DK, 2 * H])[0] for room_at in stage_room]
        xn, at = view(arena, 0, [TILES, D])
        xn_late = view(arena, at, [TILES, D])[0]
        xnT, at = view(arena, at, [DK, T])
        row_hot, at_hot = view(arena, at, [PAIRS, P], F16)
        blk_hot, at_hot = view(arena, at_hot, [PAIRS, BLOCKS])
        blk_pair, at_hot = view(arena, at_hot, [PAIRS, BLOCKS], F16)
        xb, y = [None] * 2, [None] * 2
        at = 0
        for i in range(2):
            xb[i], at = view(arena, at, [D])
            y[i], at = view(arena, at, [D])
        sa, at = view(arena, at, [H])
        g, at = view(arena, at, [H])
        y_experts = TOPK * TILES // HK
        assert LAST + y_experts <= SCATTERED - FULL + 1 and LAST * TILES * P <= (SCATTERED - LAST * 2 - FULL + 1) * HK * D
        y_in = view(w_out_words, LAST * HK * D, [TILES, TOPK, D])[0]

        wr = sb("wr", [P, DK, E])
        bias_half = sb("bias_half", [P, D])
        bo = sb("bo", [P, D])
        ident = sb("ident", [P, P])
        ident_b = sb("ident_b", [P, P], BF16)
        neg_mask = sb("neg_mask", [P, P], BF16)
        before = sb("before", [P, P], F16)
        ones = sb("ones", [P, P], F16)
        col = sb("col", [P, P])
        block_edge = sb("block_edge", [P, E])
        expert_before = sb("expert_before", [P, E, E])
        block_no = sb("block_no", [P, BLOCKS])
        pair_id = sb("pair_id", [P, PAIRS])
        trash_id = sb("trash_id", [P, BLOCKS])
        head_mask = sb("head_mask", [P, HPC])
        minus_half = sb("minus_half", [P, TILES])
        x = sb("x", [P, TILES, D])
        stats = sb("stats", [P, TILES, 6])
        mv = sb("mv", [P, TILES, 2])
        var_eps = sb("var_eps", [P, TILES])
        rstd = sb("rstd", [P, TILES])
        best = sb("best", [P, TILES, E])
        best_expert = sb("best_expert", [P, TILES, E], U32)
        choice = sb("choice", [P, TOPK, TILES, E])
        chosen = sb("chosen", [P, TILES, E], F16)
        gap = sb("gap", [P, TILES])
        e1 = sb("e1", [P, TILES])
        den = sb("den", [P, TILES])
        unread = sb("unread", [P, TILES])
        gate = sb("gate", [P, TOPK, TILES])
        tile_edge = sb("tile_edge", [P, TILES])
        live = sb("live", [P, LAST])
        gate_p = sb("gate_p", [P, LAST], I32)
        gate_q = sb("gate_q", [P, LAST], I32)
        gate_row = sb("gate_row", [P, LAST], I32)
        slot_gate = sb("slot_gate", [P, LAST])
        slot_token = sb("slot_token", [P, LAST, TILES])
        over_edge = sb("over_edge", [P, E, E])
        n_blocks = sb("n_blocks", [P, E])
        first_block = sb("first_block", [P, E])
        end_block = sb("end_block", [P, E])
        placed = sb("placed", [P, TOPK, TILES, E])
        rank = sb("rank", [P, PAIRS])
        rank_i = sb("rank_i", [P, PAIRS], I32)
        block_of = sb("block_of", [P, PAIRS])
        row_i = sb("row_i", [P, PAIRS], I32)
        blk_i = sb("blk_i", [P, PAIRS], I32)
        pair_i = sb("pair_i", [P, BLOCKS], I32)
        empty = sb("empty", [P, BLOCKS])
        scatter_row = sb("scatter_row", [P, BLOCKS], I32)
        gather_row = sb("gather_row", [P, BLOCKS], I32)
        past = sb("past", [P, BLOCKS, E])
        block_expert_f = sb("block_expert_f", [P, BLOCKS])
        block_expert = sb("block_expert", [P, BLOCKS], I32)
        neg_max = [sb(f"neg_max{u}", [P, 2, 2]) for u in range(2)]
        row_sum = placed[:, :, :, :].rearrange("p k i e -> p (k i e)")\
            .rearrange("p (b q h) -> p b q h", b=BATCH, q=2)
        inv_sum = sb("inv_sum", [P, 2, HEADS])

        x_loaded = [sem(f"x_loaded{i}") for i in range(TPAIRS)]
        router_loaded = sem("router_loaded")
        bias_loaded = sem("bias_loaded")
        attn_w_loaded = sem("attn_w_loaded")
        stage_loaded = [sem(f"stage_loaded{i}") for i in range(STAGES)]
        w_hi_ready = sem("w_hi_ready")
        w_lo_front = sem("w_lo_front")
        w_lo_back = sem("w_lo_back")
        wout_loaded = [sem(f"wout_loaded{e}") for e in range(E)]
        wout_ready = sem("wout_ready")
        xn_stored = sem("xn_stored")
        y_loaded = [sem(f"y_loaded{i}") for i in range(TPAIRS)]
        out_stored = sem("out_stored")
        const_step = sem("const_step")
        var_ready = sem("var_ready")
        rstd_ready = sem("rstd_ready")
        xn_ready = sem("xn_ready")
        xnT_in_psum = sem("xnT_in_psum")
        xnT_ready = sem("xnT_ready")
        bias_added = sem("bias_added")
        y_scaled = sem("y_scaled")
        rows_added = sem("rows_added")
        x_added = sem("x_added")
        logits_done = sem("logits_done")
        route_step = sem("route_step")
        chosen_ready = sem("chosen_ready")
        gap_ready = sem("gap_ready")
        e1_ready = sem("e1_ready")
        ranks_done = sem("ranks_done")
        hot_ready = sem("hot_ready")
        pairs_done = sem("pairs_done")
        plan_ready = sem("plan_ready")
        scatter_ready = sem("scatter_ready")
        gathered = [sem(f"gathered{u}") for u in range(2)]
        xT_in_psum = sem("xT_in_psum")
        xT_hi_ready = sem("xT_hi_ready")
        xT_lo_ready = sem("xT_lo_ready")
        a_done = sem("a_done")
        b_done = sem("b_done")
        silu_done = sem("silu_done")
        g_done = sem("g_done")
        gT_in_psum = sem("gT_in_psum")
        gT_hi_ready = sem("gT_hi_ready")
        gT_lo_ready = sem("gT_lo_ready")
        wo_hi_ready = sem("wo_hi_ready")
        wo_lo_ready = sem("wo_lo_ready")
        y_done = sem("y_done")
        y_copied = sem("y_copied")
        slots_ready = sem("slots_ready")
        gates_stored = sem("gates_stored")
        gates_gathered = sem("gates_gathered")
        slot_gate_ready = sem("slot_gate_ready")
        slot_hot_ready = sem("slot_hot_ready")
        rows_zero = sem("rows_zero")
        rows_zeroed = sem("rows_zeroed")
        gated_hi_ready = sem("gated_hi_ready")
        gated_lo_ready = sem("gated_lo_ready")
        spread_done = sem("spread_done")
        scattered = [sem(f"scattered{u}") for u in range(2)]
        v_done = sem("v_done")
        v_first_ready = sem("v_first_ready")
        v_rest_ready = sem("v_rest_ready")
        v_second_ready = sem("v_second_ready")
        v_ready = sem("v_ready")
        qk_done = sem("qk_done")
        qk_hi_ready = sem("qk_hi_ready")
        k_hi_ready = sem("k_hi_ready")
        k_lo_ready = sem("k_lo_ready")
        qk_ready = sem("qk_ready")
        k_head_ready = sem("k_head_ready")
        tail_scored = sem("tail_scored")
        head_scored = sem("head_scored")
        tail_max_done = sem("tail_max_done")
        head_max_done = sem("head_max_done")
        head_probs_ready = sem("head_probs_ready")
        tail_probs_ready = sem("tail_probs_ready")
        probsT_done = sem("probsT_done")
        pT_hi_ready = sem("pT_hi_ready")
        pT_lo_ready = sem("pT_lo_ready")
        pv_done = sem("pv_done")
        inv_ready = sem("inv_ready")
        ctx_summed = sem("ctx_summed")
        ctx_ready = sem("ctx_ready")
        ctxT_done = sem("ctxT_done")
        ctxT_ready = sem("ctxT_ready")
        o_done = sem("o_done")
        attn_added = sem("attn_added")
        stats_done = sem("stats_done")

        block = ctx.enter_context(nc.Block())

        def after_first(f, j, n):
            return f or not isinstance(j, int) or j >= n

        def y_bank(j):
            return 1 if isinstance(j, int) and j == BLOCKS - 1 else 6

        def reach(eng, signal, count):
            if not isinstance(count, int) or count > 0:
                eng.wait_ge(signal, count)

        def sweep(eng, step):
            step(0, False, True)
            with eng.Fori(1, BATCH) as b:
                step(b, True, True)
            step(BATCH, True, False)

        def divide(eng, b):
            eng.wait_ge(inv_ready, b)
            eng.wait_ge(ctx_summed, b * 2)
            for qt in range(2):
                ins = eng.tensor_tensor(ctxv[:, qt, :, :], ctxv[:, qt, :, :],
                                        bc(inv_sum[:, qt, :], 2, [P, HEADS, HD]), ALU.mult)
            ins.then_inc(ctx_ready, 1)

        def bc(ap, axis, shape):
            return ap.unsqueeze(axis).to_broadcast(shape)

        x_rows = x_in.rearrange("b (j p) d -> p (b j) d", p=P)
        out_rows = out.rearrange("b (j p) d -> p (b j) d", p=P)
        xn_rows = xn_dram.rearrange("(i p) d -> p i d", p=P)
        gate_rows = gate_dram.rearrange("(p q) o -> p (q o)", p=P)
        y_rows = y_dram[0:TOPK * T, :].rearrange("(k i p) d -> p k i d", p=P, k=TOPK)

        @block.sync
        def _(sp):
            for i in range(TPAIRS):
                rows = slice(2 * i, 2 * i + 2)
                sp.dma_start(x[:, rows, :], x_rows[:, rows, :]).then_inc(x_loaded[i], 16)
            sp.dma_start(wr[:, :, :], wr_in.rearrange("(k p) e -> p k e", p=P)).then_inc(router_loaded, 16)

            def load_w_out(e):
                sp.dma_start(w_out[:, e, :, :], wout_in[e].rearrange("(k p) n -> p k n", p=P)).then_inc(wout_loaded[e], 16)

            def pass_on_w_out(f, experts=range(E)):
                for e in experts:
                    sp.wait_ge(wout_loaded[e], 16 * (f + 1))
                    sp.sem_inc(wout_ready)

            def split(e):
                sp.wait_ge(w_hi_ready, e + 1)
                sp.wait_ge(w_lo_front, e + 1)
                sp.wait_ge(w_lo_back, e + 1)

            for e in range(E):
                if e >= STAGES:
                    split(e - STAGES)
                sp.dma_start(stage[e % STAGES][:, :, :], win_in[e].rearrange("(k p) n -> p k n", p=P))\
                    .then_inc(stage_loaded[e % STAGES], 16)
                if e == STAGES - 1:
                    sp.wait_ge(xnT_ready, TPAIRS)
            for room in range(free_experts):
                load_w_out(room)
            for e in range(E - STAGES, E):
                split(e)
                for room in range(stage_room[e % STAGES], stage_room[e % STAGES] + 2):
                    load_w_out(room)
                if e == E - STAGES:
                    pass_on_w_out(0, range(free_experts))
            for dst, src in ((bias_half, bias_in), (bo, bo_in)):
                sp.dma_start(dst[:, :], src.partition_broadcast(P)).then_inc(bias_loaded, 16)
            for f in range(2):
                if f == 0:
                    pass_on_w_out(0, range(free_experts, E))
                else:
                    sp.wait_ge(logits_done, 4)
                    for e in range(E):
                        if e == E // 2:
                            sp.wait_ge(gathered[0], 16 * (EVEN + 1))
                            sp.wait_ge(gathered[1], 16 * (ODD + 1))
                        load_w_out(e)
                    pass_on_w_out(1)
                sp.wait_ge(slots_ready, f + 1)
                sp.dma_start(gate_rows, gate[:, :, :].rearrange("p k i -> p (k i)")).then_inc(gates_stored, 16)
                sp.wait_ge(rows_zeroed, 16 * LAST * (f + 1))
                sp.wait_ge(scattered[0], 16 * S_EVEN * (f + 1))
                sp.wait_ge(scattered[1], 16 * S_ODD * (f + 1))
                for i in range(TPAIRS):
                    for k in range(TOPK):
                        sp.dma_start(y_in[:, 2 * i:2 * i + 2, k, :], y_rows[:, k, 2 * i:2 * i + 2, :])\
                            .then_inc(y_loaded[i], 16)
                if f == 0:
                    sp.wait_ge(wo_lo_ready, BLOCKS)
                    for dst, src in ((wq, wq_in), (wk, wk_in), (wv, wv_in), (wo, wo_in)):
                        sp.dma_start(dst[:, :, :], src.rearrange("(k p) n -> p k n", p=P)).then_inc(attn_w_loaded, 16)
            for i in range(0, TILES, 2):
                sp.wait_ge(x_added, TILES + i + 2)
                sp.dma_start(out_rows[:, i:i + 2, :], x[:, i:i + 2, :]).then_inc(out_stored, 16)
            sp.wait_ge(out_stored, 16 * TPAIRS)

        @block.gpsimd
        def _(pool):
            steps = [0]

            def then(ins):
                steps[0] += 1
                ins.then_inc(const_step, 1)
                pool.wait_ge(const_step, steps[0])

            def iota(t, pattern, base, mult):
                then(pool.iota(t, pattern, base=base, channel_multiplier=mult, allow_small_or_imprecise_dtypes=True))

            def select(t, pattern, base, mult, op, fill):
                then(pool.affine_select(out=t, in_=t, pattern=pattern, compare_op=op, fill=fill, base=base,
                                        channel_multiplier=mult))

            def inverse_root(phase, first=0, pairs=1):
                pool.wait_ge(var_ready, TPAIRS * phase + first + pairs)
                some = slice(2 * first, 2 * (first + pairs))
                pool.tensor_tensor(rstd[:, some], var_eps[:, some], minus_half[:, some], ALU.pow).then_inc(rstd_ready, pairs)

            then(pool.memset(ones[:, :], 1.0))
            then(pool.memset(ident[:, :], 0.0))
            select(ident[:, :], [[-1, P]], 0, 1, ALU.not_equal, 1.0)
            assert steps[0] == IDENT_CONSTS
            then(pool.memset(minus_half[:, :], -0.5))
            then(pool.memset(before[:, :], 1.0))
            select(before[:, :], [[1, P]], 0, -1, ALU.is_gt, 0.0)
            iota(block_edge[:, :], [[P, E]], 0, 0)
            then(pool.memset(expert_before[:, :, :], 1.0))
            select(expert_before[:, :, :], [[1, E], [-1, E]], 0, 0, ALU.is_gt, 0.0)
            inverse_root(0, 0)
            iota(block_no[:, :], [[1, BLOCKS]], 0, 0)
            inverse_root(0, 1)
            iota(col[:, :], [[1, P]], 0, 0)
            inverse_root(0, 2)
            iota(tile_edge[:, :], [[P, TILES]], 0, 0)
            inverse_root(0, 3)
            iota(pair_id[:, :].rearrange("p (k i) -> p k i", k=TOPK), [[T, TOPK], [P, TILES]], 1, 1)
            iota(trash_id[:, :], [[P, BLOCKS]], TOPK * T + 1, 1)
            then(pool.memset(neg_mask[:, :], 0.0))
            select(neg_mask[:, :], [[-1, P]], 0, 1, ALU.is_ge, NEG)
            then(pool.tensor_copy(ident_b[:, :], ident[:, :]))
            then(pool.memset(head_mask[:, :], 1.0))
            select(head_mask[:, :], [[-HD, HPC]], 0, 1, ALU.is_ge, 0.0)
            select(head_mask[:, :], [[HD, HPC]], HD - 1, -1, ALU.is_ge, 0.0)
            assert steps[0] == CONSTS

            def split_back(e):
                pool.wait_ge(w_hi_ready, e + 1)
                pool.tensor_tensor(w_lo[:, e, 1, :], stage[e % STAGES][:, 1, :], w_hi[:, e, 1, :].bitcast(F32),
                                   ALU.subtract).then_inc(w_lo_back, 1)

            def add_bias(phase, b, first=0, pairs=TPAIRS):
                pool.wait_ge(xn_ready, TILES * phase + 2 * (first + pairs))
                rows = x[:, 2 * first:2 * (first + pairs), :]
                pool.tensor_tensor(rows, rows, bc(b[:, :], 1, [P, 2 * pairs, D]), ALU.add).then_inc(bias_added, pairs)

            def gather(f, j):
                if f or j >= 2:
                    pool.wait_ge(xT_in_psum, f * BLOCKS + max(j - 1, 0))
                pool.indirect_dma_start(out=xb[j % 2][:, :], out_offset=None, in_=xn_dram,
                                        in_offset=bass.IndirectOffsetOnAxis(ap=gather_row[:, j:j + 1], axis=0))\
                    .then_inc(gathered[j % 2], 16)

            def scatter(f, j):
                pool.wait_ge(y_copied, f * SCATTERED + j + 1)
                pool.indirect_dma_start(out=y_dram, in_=y[j % 2][:, :], in_offset=None,
                                        out_offset=bass.IndirectOffsetOnAxis(ap=scatter_row[:, j:j + 1], axis=0))\
                    .then_inc(scattered[j % 2], 16)

            def zero_rows(f):
                pool.memset(y[1][:, :], 0.0).then_inc(rows_zero, 1)
                pool.wait_ge(scatter_ready, f + 1)
                pool.wait_ge(rows_zero, f + 1)
                for j in range(SCATTERED, BLOCKS):
                    pool.indirect_dma_start(out=y_dram, in_=y[1][:, :], in_offset=None,
                                            out_offset=bass.IndirectOffsetOnAxis(ap=scatter_row[:, j:j + 1], axis=0))\
                        .then_inc(rows_zeroed, 16)

            def gather_gates(f):
                pool.wait_ge(gates_stored, 16 * (f + 1))
                for k in range(LAST):
                    pool.indirect_dma_start(out=slot_gate[:, k:k + 1], out_offset=None, in_=gate_dram,
                                            in_offset=bass.IndirectOffsetOnAxis(ap=gate_row[:, k:k + 1], axis=0))\
                        .then_inc(gates_gathered, 16)

            def mark_tokens(f, k, half):
                if half == 0:
                    pool.wait_ge(wo_lo_ready, f * BLOCKS + FULL - 1 + LAST)
                for t in range(half * TILES // 2, (half + 1) * TILES // 2):
                    ins = pool.tensor_scalar(slot_hot[k][:, t, :], col[:, :], slot_token[:, k, t:t + 1], None, ALU.is_equal)
                ins.then_inc(slot_hot_ready, 1)

            def ffn(f):
                if f == 0:
                    for e in range(TURN_AFTER):
                        split_back(e)
                pool.wait_ge(plan_ready, f + 1)
                pool.wait_ge(xn_stored, 16 * (f + 1))
                if f:
                    for i in range(TPAIRS):
                        pool.wait_ge(y_loaded[i], 16 * TOPK)
                for j in range(AHEAD):
                    if f == 0 and j == 2:
                        split_back(TURN_AFTER)
                    elif f == 0 and j == 3:
                        for e in range(TURN_AFTER + 1, E):
                            split_back(e)
                    gather(f, j)
                zero_rows(f)
                for j in range(SCATTERED):
                    if j + AHEAD < BLOCKS:
                        gather(f, j + AHEAD)
                    scatter(f, j)
                    if j == 6:
                        if f == 0:
                            pool.wait_ge(bias_loaded, 32)
                            then(pool.tensor_scalar(bias_half[:, :], bias_half[:, :], 0.5, None, ALU.mult))
                        add_bias(2 * f, bias_half)
                    elif j == SCATTERED // 2:
                        gather_gates(f)
                    elif j == SCATTERED // 2 + 2:
                        pool.wait_ge(gates_gathered, 16 * LAST * (f + 1))
                        pool.tensor_tensor(slot_gate[:, :], slot_gate[:, :], live[:, :], ALU.mult).then_inc(slot_gate_ready, 1)
                    half = j - (SCATTERED - 2 * LAST)
                    if half >= 0:
                        mark_tokens(f, half // 2, half % 2)

            ffn(0)
            pool.wait_ge(bias_added, TPAIRS)
            for i in range(TPAIRS):
                inverse_root(1, i)
                if 1 <= i < TPAIRS - 1:
                    add_bias(1, bo, i - 1, 1)

            def mask_keys(b, s):
                g = b * HPAIRS + (s - SLAG)
                p = (s - SLAG) % HPAIRS
                c = p // CPAIRS
                chunks = (b * DK + (c + 1 - (DK if s < SLAG else 0)))
                reach(pool, head_scored, g + (1 - KSLOTS))
                for part, (k, ready) in enumerate(((k_hi, k_hi_ready), (k_lo, k_lo_ready))):
                    pool.wait_ge(ready, chunks)
                    for hh in range(2):
                        h = 2 * p + hh
                        ins = pool.tensor_tensor(k_head[s % KSLOTS][:, part, hh, :], k[:, c, :].bitcast(F32),
                                                 head_mask[:, h % HPC:h % HPC + 1].to_broadcast([P, SEQ]), ALU.mult)
                ins.then_inc(k_head_ready, 1)

            def step(b, old, new):
                for s in range(HPAIRS):
                    if old if s < SLAG else new:
                        mask_keys(b, s)
                    if old and new and s == SUM_STEP + POOL_LEAD:
                        divide(pool, b)
                    if not old and s == BIAS_STEP:
                        add_bias(1, bo, TPAIRS - 2, 2)

            sweep(pool, step)
            inverse_root(2, 0, TPAIRS - 1)
            inverse_root(2, TPAIRS - 1)
            ffn(1)

        @block.scalar
        def _(act):
            def turn_out(phase, pairs=range(TPAIRS)):
                to = xnT_late if phase == 2 else xnT
                for pair in pairs:
                    act.wait_ge(xnT_in_psum, 4 * phase + pair + 1)
                    act.activation(to[:, :, pair * 256:(pair + 1) * 256],
                                   bank[pair % 2][:, :].rearrange("p (k t) -> p k t", k=DK), ACT.Copy)\
                        .then_inc(xnT_ready, 1)

            def scale_rows(f):
                for i, k in PE_ROWS[f]:
                    act.wait_ge(y_loaded[i], 16 * TOPK * (f + 1))
                    for t in (2 * i, 2 * i + 1):
                        ins = act.activation(y_in[:, t, k, :], y_in[:, t, k, :], ACT.Copy, scale=gate[:, k, t:t + 1])
                    ins.then_inc(y_scaled, 1)

            def split_front(e):
                act.wait_ge(stage_loaded[e % STAGES], 16 * (e // STAGES + 1))
                act.activation(w_hi[:, e, :, :], stage[e % STAGES][:, :, :], ACT.Copy).then_inc(w_hi_ready, 1)

            def copy_xT(f, j, u):
                act.wait_ge(xT_in_psum, f * BLOCKS + j + 1)
                if after_first(f, j, 2):
                    act.wait_ge(b_done, f * BLOCKS + j - 1)
                act.activation(xT_hi[u][:, :, :], bank[5][:, 0:D].rearrange("p (k t) -> p k t", k=DK), ACT.Copy)\
                    .then_inc(xT_hi_ready, 1)

            def silu(f, j, u):
                act.wait_ge(a_done, f * BLOCKS + j + 1)
                if after_first(f, j, 1):
                    act.wait_ge(g_done, f * BLOCKS + j)
                act.activation(sa[:, :], bank[u][:, :], ACT.Silu).then_inc(silu_done, 1)

            def copy_gT(f, j):
                act.wait_ge(gT_in_psum, f * BLOCKS + j + 1)
                if after_first(f, j, 1):
                    act.wait_ge(y_done, f * BLOCKS + j)
                act.activation(gT_hi[:, :, :], bank[4][:, :].rearrange("p (c t) -> p c t", c=HK), ACT.Copy)\
                    .then_inc(gT_hi_ready, 1)

            def split_out(f, j, u):
                e = act.value_load(block_expert[0:1, bass.ds(j, 1)], min_val=0, max_val=E - 1)
                act.wait_ge(wout_ready, e + (f * E + 1))
                if after_first(f, j, 2):
                    act.wait_ge(y_done, f * BLOCKS + j - 1)
                act.activation(wo_hi[u][:, :, :], w_out[:, bass.ds(e, 1), :, :].rearrange("p o c d -> p (o c) d"), ACT.Copy)\
                    .then_inc(wo_hi_ready, 1)

            def copy_y(f, j, u, scatters_before):
                act.wait_ge(y_done, f * BLOCKS + j + 1)
                if not isinstance(scatters_before, int) or scatters_before:
                    act.wait_ge(scattered[u], scatters_before * 16)
                if isinstance(j, int) and j == 1:
                    act.wait_ge(rows_zeroed, 16 * LAST * (f + 1))
                act.activation(y[u][:, :], bank[6][:, 0:D], ACT.Copy).then_inc(y_copied, 1)

            def gate_y(f, j):
                act.wait_ge(y_done, f * BLOCKS + j + 1)
                act.wait_ge(slot_gate_ready, f + 1)
                k = j - SCATTERED
                act.activation(gated_rows[k][0][:, :], bank[y_bank(j)][:, 0:D], ACT.Copy, scale=slot_gate[:, k:k + 1])\
                    .then_inc(gated_hi_ready, 1)

            def ffn(f):
                if f == 0:
                    turn_out(0, range(TPAIRS - 1))
                    split_front(0)
                act.wait_ge(xn_ready, TILES * (2 * f + 1))
                act.dma_start(xn_rows, (xn_late if f else xn)[:, :, :]).then_inc(xn_stored, 16)
                turn_out(2 * f, (TPAIRS - 1,))
                if f == 0:
                    for e in range(1, STAGES):
                        split_front(e)
                act.wait_ge(gap_ready, f + 1)
                act.activation(e1[:, :], gap[:, :], ACT.Exp).then_inc(e1_ready, 1)
                act.activation(unread[:, :], gap[:, :], ACT.Silu)
                base = (S_EVEN * f, S_ODD * f)
                if f == 0:
                    for e in range(STAGES, TURN_AFTER + 1):
                        split_front(e)
                copy_xT(f, 0, 0)
                if f == 0:
                    for e in range(TURN_AFTER + 1, E):
                        split_front(e)
                silu(f, 0, 0)
                copy_xT(f, 1, 1)
                act.wait_ge(plan_ready, f + 1)
                split_out(f, 0, 0)

                def body(j, u, of_parity, silu_next=True, copy_next=True):
                    if silu_next:
                        silu(f, j + 1, 1 - u)
                    copy_gT(f, j)
                    if silu_next:
                        split_out(f, j + 1, 1 - u)
                    if copy_next:
                        copy_xT(f, j + 2, u)
                    if isinstance(j, int) and j >= SCATTERED:
                        gate_y(f, j)
                    else:
                        copy_y(f, j, u, of_parity + base[u])

                for j in range(PEELED):
                    body(j, j % 2, j // 2)
                with act.Fori(0, LOOPED) as i:
                    for u in range(2):
                        body(i * 2 + (PEELED + u), (PEELED + u) % 2, i + (PEELED + u) // 2)
                for j in range(AFTER, BLOCKS):
                    body(j, j % 2, j // 2, j + 1 < BLOCKS, j + 2 < BLOCKS)

            ffn(0)
            scale_rows(0)
            act.activation(e1[:, :], gap[:, :], ACT.Exp)
            turn_out(1, (0,))
            act.wait_ge(x_added, TILES)

            def chunk(b, c):
                act.wait_ge(qk_done, b * DK + (c + 1))
                reach(act, head_scored, b * HPAIRS + (CPAIRS * (c + 1) - HPAIRS))
                act.activation(k_hi[:, c, :], bank[7][:, SEQ:2 * SEQ], ACT.Copy).then_inc(k_hi_ready, 1)
                act.activation(q_hi[c][:, :, :], bank[7][:, 0:SEQ].rearrange("p (q t) -> p q t", q=2), ACT.Copy,
                               scale=1.0 / SEQ ** 0.5).then_inc(qk_hi_ready, 1)

            def exps(b, s, tail):
                g = b * HPAIRS + (s - SLAG)
                p, u = (s - SLAG) % HPAIRS, s % 2
                batch = b if s >= SLAG else b - 1
                if tail:
                    act.wait_ge(tail_max_done, g + 1)
                    reach(act, probsT_done, g * 2 - 2)
                    for hh in range(2):
                        h = 2 * p + hh
                        act.activation(probs[u][:, hh, 1:3, :],
                                       bank[u][:, hh * SEQ:(hh + 1) * SEQ].rearrange("p (k t) -> p k t", k=2), ACT.Exp,
                                       bias=neg_max[u][:, 1, hh:hh + 1],
                                       accum_out=row_sum[:, bass.ds(batch, 1), 1, h:h + 1]).then_inc(tail_probs_ready, 1)
                    return
                act.wait_ge(head_max_done, g + 1)
                for hh in range(2):
                    h = 2 * p + hh
                    act.activation(probs[u][:, hh, 0, :], bank[2][:, P * hh:P * (hh + 1)], ACT.Exp,
                                   bias=neg_max[u][:, 0, hh:hh + 1],
                                   accum_out=row_sum[:, bass.ds(batch, 1), 0, h:h + 1]).then_inc(head_probs_ready, 1)

            def high(b, s):
                g = b * HPAIRS + (s - SLAG - 1)
                for hh in range(2):
                    act.wait_ge(probsT_done, g * 2 + (hh + 1))
                    reach(act, pv_done, g * 2 + (hh - 3))
                    act.activation(pT_hi[(s - 1) % 2 * 2 + hh][:, :, :],
                                   bank[3 + hh][:, 0:3 * P].rearrange("p (k t) -> p k t", k=3),
                                   ACT.Copy, scale=P_SCALE).then_inc(pT_hi_ready, 1)

            def step(b, old, new):
                for s in range(HPAIRS):
                    if not new and s == SUM_STEP:
                        turn_out(2, range(1))
                    if old and s == OUT_STEP:
                        act.wait_ge(ctxT_done, b)
                        act.activation(ctxT[:, :, :], bank[7][:, :].rearrange("p (k t) -> p k t", k=DK), ACT.Copy,
                                       scale=1.0 / P_SCALE).then_inc(ctxT_ready, 1)
                        if not new:
                            turn_out(2, range(1, TPAIRS - 1))
                    if old if s < SLAG else new:
                        exps(b, s, True)
                    if not old and s == 0:
                        turn_out(1, (1,))
                    if new and s in CHUNK_STEP:
                        chunk(b, CHUNK_STEP.index(s))
                    if old if s < SLAG else new:
                        exps(b, s, False)
                    if not old and s == 0:
                        turn_out(1, (2,))
                    if s in VALUES and not old:
                        first, last = VALUES[s]
                        for t in range(first, last + 1):
                            if t < last:
                                act.wait_ge(v_done, t + 1)
                                act.activation(v[:, t, :, 0:HD],
                                               bank[VBANK[t]][:, 0:D].rearrange("p (h d) -> p h d", h=HEADS),
                                               ACT.Copy).then_inc(v_first_ready, 1)
                            if s == 1 and t == first:
                                turn_out(1, (3,))
                            if t > first:
                                act.wait_ge(v_rest_ready, t)
                                act.activation(v[:, t - 1, :, HD:2 * HD], v_rest[(t - 1) % VSLOTS][:, :, :], ACT.Copy)\
                                    .then_inc(v_second_ready, 1)
                    if old if s < SLAG + 1 else new:
                        high(b, s)

            sweep(act, step)
            ffn(1)
            scale_rows(1)

        @block.vector
        def _(dve):
            steps = [0]

            def mark(ins):
                steps[0] += 1
                ins.then_inc(route_step, 1)
                return steps[0]

            def then(ins):
                dve.wait_ge(route_step, mark(ins))

            def measure(phase, i):
                two = slice(2 * i, 2 * i + 2)
                if phase == 0:
                    dve.wait_ge(x_loaded[i], 16)
                dve.bn_stats(stats[:, 2 * i, :], x[:, 2 * i, :])
                then(dve.bn_stats(stats[:, 2 * i + 1, :], x[:, 2 * i + 1, :]))
                dve.bn_aggr(mv[:, 2 * i, :], stats[:, 2 * i, :])
                then(dve.bn_aggr(mv[:, 2 * i + 1, :], stats[:, 2 * i + 1, :]))
                dve.tensor_scalar(var_eps[:, two], mv[:, two, 1], EPS, None, ALU.add).then_inc(var_ready, 1)

            def scale(phase, i):
                to = xn_late if phase == 2 else xn
                dve.wait_ge(rstd_ready, TPAIRS * phase + i + 1)
                for t in (2 * i, 2 * i + 1):
                    dve.tensor_scalar(to[:, t, :], x[:, t, :], mv[:, t, 0:1], rstd[:, t:t + 1], ALU.subtract, ALU.mult)\
                        .then_inc(xn_ready, 1)

            def normalise(phase):
                for i in range(TPAIRS + 1):
                    if i < TPAIRS:
                        measure(phase, i)
                    if i >= 1:
                        scale(phase, i - 1)

            def split_low(e):
                dve.wait_ge(w_hi_ready, e + 1)
                dve.tensor_tensor(w_lo[:, e, 0, :], stage[e % STAGES][:, 0, :], w_hi[:, e, 0, :].bitcast(F32),
                                  ALU.subtract).then_inc(w_lo_front, 1)

            def route(f):
                te = [P, TILES, E]
                if f == 0:
                    split_low(0)
                for n, tiles in enumerate((range(TILES - 2), range(TILES - 2, TILES))):
                    dve.wait_ge(logits_done, 2 * f + n + 1)
                    logits = bank[LBANK[n]][:, 0:TILES * E].rearrange("p (i e) -> p i e", e=E)
                    for i in tiles:
                        ins = dve.max(best[:, i, :], logits[:, i, :])
                    then(ins)
                    for i in tiles:
                        ins = dve.max_index(best_expert[:, i, :], best[:, i, :], logits[:, i, :])
                    then(ins)
                    some = slice(tiles[0], tiles[-1] + 1)
                    both = [P, TOPK, len(tiles), E]
                    ins = dve.tensor_tensor(choice[:, :, some, :],
                                            best_expert[:, some, 0:TOPK].rearrange("p i k -> p k i").unsqueeze(3).to_broadcast(both),
                                            block_no[:, 0:E].unsqueeze(1).unsqueeze(1).to_broadcast(both), ALU.is_equal)
                then(ins)
                dve.tensor_tensor(chosen[:, :, :], choice[:, 0, :, :], choice[:, 1, :, :], ALU.add).then_inc(chosen_ready, 1)
                if f == 0:
                    split_low(1)
                dve.tensor_tensor(gap[:, :], best[:, :, 1], best[:, :, 0], ALU.subtract).then_inc(gap_ready, 1)
                both = [P, TOPK, TILES, E]
                pairs = "p k i e -> p (k i) e"
                ranks = bank[4][:, 0:TILES * E].rearrange("p (i e) -> p i e", e=E)
                dve.wait_ge(ranks_done, f + 1)
                placed_at = mark(dve.tensor_tensor(placed[:, :, :, :], choice[:, :, :, :], bc(ranks, 1, both), ALU.mult))
                over_at = mark(dve.tensor_tensor(over_edge[:, :, :], bc(bank[6][:, 0:E], 2, [P, E, E]),
                                                 bc(block_edge[:, :], 1, [P, E, E]), ALU.is_gt))
                dve.wait_ge(route_step, placed_at)
                rank_at = mark(dve.tensor_reduce(rank[:, :].rearrange("p (k i) -> p k i", k=TOPK), placed[:, :, :, :],
                                                 AX_X, ALU.add))
                dve.wait_ge(route_step, over_at)
                blocks_at = mark(dve.tensor_reduce(n_blocks[:, :], over_edge[:, :, :], AX_X, ALU.add))
                dve.wait_ge(route_step, rank_at)
                rank_at = mark(dve.tensor_copy(rank_i[:, :], rank[:, :]))
                dve.wait_ge(route_step, blocks_at)
                over_at = mark(dve.tensor_tensor(over_edge[:, :, :], expert_before[:, :, :],
                                                 bc(n_blocks[:, :], 1, [P, E, E]), ALU.mult))
                dve.wait_ge(route_step, rank_at)
                dve.tensor_scalar(blk_i[:, :], rank_i[:, :], P.bit_length() - 1, None, ALU.logical_shift_right)
                row_at = mark(dve.tensor_scalar(row_i[:, :], rank_i[:, :], P - 1, None, ALU.bitwise_and))
                dve.wait_ge(route_step, over_at)
                first_at = mark(dve.tensor_reduce(first_block[:, :], over_edge[:, :, :], AX_X, ALU.add))

                def one_hot_rows(q):
                    shape = [P, q.stop - q.start, P]
                    return mark(dve.tensor_tensor(row_hot[:, q, :], bc(row_i[:, q], 2, shape), bc(col[:, :], 1, shape),
                                                  ALU.is_equal))

                dve.wait_ge(route_step, row_at)
                if f == 0:
                    split_low(2)
                one_hot_rows(slice(0, PAIRS // 2))
                dve.wait_ge(route_step, first_at)
                placed_at = mark(dve.tensor_tensor(placed[:, :, :, :], choice[:, :, :, :],
                                                   first_block[:, :].unsqueeze(1).unsqueeze(1).to_broadcast(both), ALU.mult))
                end_at = mark(dve.tensor_tensor(end_block[:, :], first_block[:, :], n_blocks[:, :], ALU.add))
                dve.wait_ge(route_step, placed_at)
                block_at = mark(dve.tensor_reduce(block_of[:, :].rearrange("p (k i) -> p k i", k=TOPK), placed[:, :, :, :],
                                                  AX_X, ALU.add))
                one_hot_rows(slice(PAIRS // 2, PAIRS))
                if f == 0:
                    split_low(3)
                dve.wait_ge(route_step, block_at)
                block_at = mark(dve.tensor_tensor(block_of[:, :], block_of[:, :], blk_i[:, :], ALU.add))
                dve.wait_ge(route_step, end_at)
                past_at = mark(dve.tensor_tensor(past[:, :, :], bc(end_block[:, :], 1, [P, BLOCKS, E]),
                                                 bc(block_no[:, :], 2, [P, BLOCKS, E]), ALU.is_le))
                dve.wait_ge(route_step, block_at)
                then(dve.tensor_tensor(blk_hot[:, :, :], bc(block_of[:, :], 2, [P, PAIRS, BLOCKS]),
                                       bc(block_no[:, :], 1, [P, PAIRS, BLOCKS]), ALU.is_equal))
                dve.tensor_tensor(blk_pair[:, :, :], blk_hot[:, :, :], bc(pair_id[:, :], 2, [P, PAIRS, BLOCKS]), ALU.mult)\
                    .then_inc(hot_ready, 1)
                dve.wait_ge(route_step, past_at)
                then(dve.tensor_reduce(block_expert_f[:, :], past[:, :, :], AX_X, ALU.add))
                dve.tensor_scalar(block_expert[:, :], block_expert_f[:, :], float(E - 1), None, ALU.min)
                dve.wait_ge(pairs_done, f + 1)
                pair_of = bank[7][:, 0:BLOCKS]
                then(dve.tensor_scalar(pair_i[:, :], pair_of, 1.0, 1.0, ALU.max, ALU.subtract))
                dve.tensor_scalar(gather_row[:, :], pair_i[:, :], T - 1, None, ALU.bitwise_and).then_inc(plan_ready, 1)
                then(dve.scalar_tensor_tensor(empty[:, :], pair_of, 0.0, trash_id[:, :], ALU.is_equal, ALU.mult))
                dve.scalar_tensor_tensor(scatter_row[:, :], pair_of, 1.0, empty[:, :], ALU.subtract, ALU.add)\
                    .then_inc(scatter_ready, 1)
                if f == 0:
                    split_low(STAGES + 1)
                dve.wait_ge(e1_ready, f + 1)
                then(dve.tensor_scalar(den[:, :], e1[:, :], 1.0, None, ALU.add))
                then(dve.reciprocal(den[:, :], den[:, :]))
                then(dve.tensor_scalar(gate[:, 0, :], den[:, :], 0.5, None, ALU.mult))
                then(dve.tensor_tensor(gate[:, 1, :], gate[:, 0, :], e1[:, :], ALU.mult))
                dve.tensor_scalar(live[:, :], pair_of[:, SCATTERED:BLOCKS], 0.0, None, ALU.is_gt)
                dve.tensor_scalar(gate_p[:, :], pair_i[:, SCATTERED:BLOCKS], P - 1, PAIRS.bit_length() - 1, ALU.bitwise_and,
                                  ALU.logical_shift_left)
                dve.tensor_scalar(gate_q[:, :], pair_i[:, SCATTERED:BLOCKS], P.bit_length() - 1, None, ALU.logical_shift_right)
                each = [P, LAST, TILES]
                then(dve.tensor_tensor(slot_token[:, :, :], bc(gather_row[:, SCATTERED:BLOCKS], 2, each),
                                       bc(tile_edge[:, :], 1, each), ALU.subtract))
                dve.tensor_tensor(gate_row[:, :], gate_p[:, :], gate_q[:, :], ALU.bitwise_or).then_inc(slots_ready, 1)

            def copy_xT_low(f, j, u):
                dve.wait_ge(xT_hi_ready, f * BLOCKS + j + 1)
                if after_first(f, j, 2):
                    dve.wait_ge(b_done, f * BLOCKS + j - 1)
                dve.tensor_tensor(xT_lo[u][:, :, :], bank[5][:, 0:D].rearrange("p (k t) -> p k t", k=DK),
                                  xT_hi[u][:, :, :].bitcast(F32), ALU.subtract).then_inc(xT_lo_ready, 1)

            def expert(j):
                return dve.value_load(block_expert[0:1, bass.ds(j, 1)], min_val=0, max_val=E - 1)

            def split_out_low(f, j, u, e):
                dve.wait_ge(wo_hi_ready, f * BLOCKS + j + 1)
                if after_first(f, j, 1):
                    dve.wait_ge(y_done, f * BLOCKS + j)
                dve.tensor_tensor(wo_lo[:, :, :], w_out[:, bass.ds(e, 1), :, :].rearrange("p o c d -> p (o c) d"),
                                  wo_hi[u][:, :, :].bitcast(F32), ALU.subtract).then_inc(wo_lo_ready, 1)

            def copy_gT_low(f, j):
                dve.wait_ge(gT_hi_ready, f * BLOCKS + j + 1)
                dve.tensor_tensor(gT_lo[:, :, :], bank[4][:, :].rearrange("p (c t) -> p c t", c=HK),
                                  gT_hi[:, :, :].bitcast(F32), ALU.subtract).then_inc(gT_lo_ready, 1)

            def gated(f, j, u):
                dve.wait_ge(b_done, f * BLOCKS + j + 1)
                dve.wait_ge(silu_done, f * BLOCKS + j + 1)
                if after_first(f, j, 1):
                    dve.wait_ge(gT_in_psum, f * BLOCKS + j)
                dve.tensor_tensor(g[:, :], sa[:, :], bank[2 + u][:, :], ALU.mult).then_inc(g_done, 1)

            def gate_y_low(f, j):
                k = j - SCATTERED
                dve.wait_ge(gated_hi_ready, f * LAST + k + 1)
                dve.scalar_tensor_tensor(gated_rows[k][1][:, :], bank[y_bank(j)][:, 0:D], slot_gate[:, k:k + 1],
                                         gated_rows[k][0][:, :].bitcast(F32), ALU.mult, ALU.subtract).then_inc(gated_lo_ready, 1)

            def add_rows(f, i, k):
                dve.wait_ge(y_loaded[i], 16 * TOPK * (f + 1))
                n = DVE_ROWS[f].index((i, k))
                if n:
                    dve.wait_ge(rows_added, f * len(DVE_ROWS[0]) + n)
                for t in (2 * i, 2 * i + 1):
                    ins = dve.scalar_tensor_tensor(x[:, t, :], y_in[:, t, k, :], gate[:, k, t:t + 1], x[:, t, :],
                                                   ALU.mult, ALU.add)
                ins.then_inc(rows_added, 1)

            def settle(f, i):
                before = [n + 1 for n, (pair, k) in enumerate(DVE_ROWS[f]) if pair == i]
                if before:
                    dve.wait_ge(rows_added, f * len(DVE_ROWS[0]) + max(before))
                dve.wait_ge(spread_done, TPAIRS * f + i + 1)
                two = x[:, 2 * i:2 * i + 2, :].rearrange("p i d -> p (i d)")
                dve.tensor_tensor(two, two, bank[ACC_BANK[i]][:, :], ALU.add).then_inc(x_added, 2)

            def settle_all(f):
                settle(f, 0)
                for i in range(TPAIRS):
                    if f == 0:
                        dve.wait_ge(x_added, 2 * i + 2)
                        dve.bn_stats(stats[:, 2 * i, :], x[:, 2 * i, :])
                        measured = mark(dve.bn_stats(stats[:, 2 * i + 1, :], x[:, 2 * i + 1, :]))
                    for pair, k in DVE_ROWS[f]:
                        if pair == i + 2:
                            add_rows(f, pair, k)
                    if i + 1 < TPAIRS:
                        settle(f, i + 1)
                    if f == 0:
                        two = slice(2 * i, 2 * i + 2)
                        dve.wait_ge(route_step, measured)
                        dve.bn_aggr(mv[:, 2 * i, :], stats[:, 2 * i, :])
                        measured = mark(dve.bn_aggr(mv[:, 2 * i + 1, :], stats[:, 2 * i + 1, :]))
                        if i >= 1:
                            scale(1, i - 1)
                        dve.wait_ge(route_step, measured)
                        dve.tensor_scalar(var_eps[:, two], mv[:, two, 1], EPS, None, ALU.add).then_inc(var_ready, 1)

            def ffn(f):
                route(f)
                if f == 0:
                    split_low(TURN_AFTER)
                copy_xT_low(f, 0, 0)
                if f == 0:
                    for e in range(TURN_AFTER + 1, E):
                        split_low(e)
                copy_xT_low(f, 1, 1)
                first = expert(0)
                gated(f, 0, 0)
                split_out_low(f, 0, 0, first)

                def body(j, u, gate_next=True, copy_next=True):
                    if gate_next:
                        e = expert(j + 1)
                    copy_gT_low(f, j)
                    if copy_next:
                        copy_xT_low(f, j + 2, u)
                    if gate_next:
                        gated(f, j + 1, 1 - u)
                        split_out_low(f, j + 1, 1 - u, e)

                for j in range(PEELED):
                    body(j, j % 2)
                with dve.Fori(0, LOOPED) as i:
                    for u in range(2):
                        body(i * 2 + (PEELED + u), (PEELED + u) % 2)
                for j in range(AFTER, BLOCKS):
                    body(j, j % 2, j + 1 < BLOCKS, j + 2 < BLOCKS)
                gate_y_low(f, SCATTERED)
                dve.wait_ge(bias_added, TPAIRS * (2 * f + 1))
                add_rows(f, 0, 0)
                gate_y_low(f, SCATTERED + 1)
                add_rows(f, 0, 1)
                add_rows(f, 1, 0)
                settle_all(f)

            normalise(0)
            ffn(0)
            scale(1, TPAIRS - 1)

            def chunk(b, c):
                dve.wait_ge(qk_hi_ready, b * DK + (c + 1))
                dve.tensor_tensor(k_lo[:, c, :], bank[7][:, SEQ:2 * SEQ], k_hi[:, c, :].bitcast(F32), ALU.subtract)\
                    .then_inc(k_lo_ready, 1)
                dve.scalar_tensor_tensor(q_lo[c][:, :, :], bank[7][:, 0:SEQ].rearrange("p (q t) -> p q t", q=2),
                                         1.0 / SEQ ** 0.5, q_hi[c][:, :, :].bitcast(F32),
                                         ALU.mult, ALU.subtract).then_inc(qk_ready, 1)

            def maxima(b, s, tail):
                g = b * HPAIRS + (s - SLAG)
                u = s % 2
                if tail:
                    dve.wait_ge(tail_scored, g + 1)
                    reach(dve, tail_probs_ready, g * 2 - 2)
                    dve.tensor_reduce(neg_max[u][:, 1, :], bank[u][:, :].rearrange("p (h k) -> p h k", h=2),
                                      AX_X, ALU.max, negate=True).then_inc(tail_max_done, 1)
                else:
                    dve.wait_ge(head_scored, g + 1)
                    dve.tensor_reduce(neg_max[u][:, 0, :], bank[2][:, 0:2 * P].rearrange("p (h k) -> p h k", h=2),
                                      AX_X, ALU.max, negate=True).then_inc(head_max_done, 1)

            def low(b, s):
                g = b * HPAIRS + (s - SLAG - 2)
                for hh in range(2):
                    u = s % 2 * 2 + hh
                    dve.wait_ge(pT_hi_ready, g * 2 + (hh + 1))
                    dve.scalar_tensor_tensor(pT_lo[u][:, :, :], bank[3 + hh][:, 0:3 * P].rearrange("p (k t) -> p k t", k=3),
                                             P_SCALE, pT_hi[u][:, :, :], ALU.mult, ALU.subtract).then_inc(pT_lo_ready, 1)

            def add_up(b):
                sums = row_sum[:, bass.ds(b - 1, 1), :, :].rearrange("p o q h -> p (o q) h")
                dve.wait_ge(pv_done, b * HEADS)
                for qt in range(2):
                    dve.tensor_reduce(ctxv[:, qt, :, :], bank[5 + qt][:, :].rearrange("p (h w d) -> p h d w", w=2, d=HD),
                                      AX_X, ALU.add).then_inc(ctx_summed, 1)
                dve.reciprocal(inv_sum[:, :, :], sums).then_inc(inv_ready, 1)

            def add_attention(b):
                dve.wait_ge(o_done, b)
                rows = x[:, bass.ds(b * 2 - 2, 2), :]
                dve.tensor_tensor(rows, rows, bank[7][:, :].rearrange("p (q d) -> p q d", q=2), ALU.add)\
                    .then_inc(attn_added, 1)

            def measure_batch(b):
                dve.wait_ge(attn_added, b + 2)
                for t in (2 * b, 2 * b + 1):
                    ins = dve.bn_stats(stats[:, t, :], x[:, t, :])
                ins.then_inc(stats_done, 1)

            def sum_up(first, pairs):
                dve.wait_ge(stats_done, first + pairs)
                tiles = slice(2 * first, 2 * (first + pairs))
                for t in range(2 * first, 2 * (first + pairs)):
                    ins = dve.bn_aggr(mv[:, t, :], stats[:, t, :])
                then(ins)
                dve.tensor_scalar(var_eps[:, tiles], mv[:, tiles, 1], EPS, None, ALU.add).then_inc(var_ready, pairs)

            def step(b, old, new):
                for s in range(HPAIRS):
                    if old and s == SUM_STEP:
                        add_up(b)
                    if old if s < SLAG else new:
                        maxima(b, s, True)
                    if s in CHUNK_STEP and (old if s < SLAG + 2 else new):
                        low(b, s)
                    if old if s < SLAG else new:
                        maxima(b, s, False)
                    if new and s in CHUNK_STEP:
                        chunk(b, CHUNK_STEP.index(s))
                    if not new and s == SUM_STEP:
                        divide(dve, b)
                        scale(2, 1)
                        scale(2, 2)
                    if s not in CHUNK_STEP and (old if s < SLAG + 2 else new):
                        low(b, s)
                    if not new and s < BATCH - 1:
                        measure_batch(s)
                        if s == BATCH - 2:
                            sum_up(0, BATCH - 1)
                    if not new and s == SUM_STEP - 1:
                        scale(2, 0)
                    if s in VALUES and not old:
                        for t in range(*VALUES[s]):
                            dve.wait_ge(v_first_ready, t + 1)
                            reach(dve, v_ready, t + 1 - VSLOTS)
                            dve.tensor_tensor(v_rest[t % VSLOTS][:, :, :],
                                              bank[VBANK[t]][:, 0:D].rearrange("p (h d) -> p h d", h=HEADS),
                                              v[:, t, :, 0:HD], ALU.subtract).then_inc(v_rest_ready, 1)
                    if s in THIRDS and not old:
                        for t in range(*THIRDS[s]):
                            dve.wait_ge(v_second_ready, t + 1)
                            dve.tensor_tensor(v[:, t, :, 2 * HD:3 * HD], v_rest[t % VSLOTS][:, :, :], v[:, t, :, HD:2 * HD],
                                              ALU.subtract).then_inc(v_ready, 1)
                    if s == OUT_STEP + 1:
                        if old:
                            add_attention(b)
                        else:
                            dve.wait_ge(bias_added, 2 * TPAIRS)
                            dve.sem_inc(attn_added, 1)

            sweep(dve, step)
            measure_batch(BATCH - 1)
            sum_up(TPAIRS - 1, 1)
            scale(2, TPAIRS - 1)
            ffn(1)

        @block.tensor
        def _(pe):
            def warm(n, into=5):
                for _ in range(n):
                    pe.matmul(bank[into][:, :], ones[:, :], bc(ones[:, :], 1, [P, 512 // P, P]), start=True, stop=True)

            def turn(phase, pairs=range(TPAIRS)):
                source = xn_late if phase == 2 else xn
                for pair in pairs:
                    pe.wait_ge(xn_ready, TILES * phase + 2 * pair + 2)
                    if pair >= 2:
                        pe.wait_ge(xnT_ready, 4 * phase + pair - 1)
                    for k in range(DK):
                        for i in range(2):
                            at = k * 256 + i * P
                            last = pe.transpose(bank[pair % 2][:, at:at + P], source[:, 2 * pair + i, k * P:(k + 1) * P],
                                                ident[:, :])
                    last.then_inc(xnT_in_psum, 1)

            def score_experts(f, pairs):
                source = xnT_late if f else xnT
                for pair in pairs:
                    pe.wait_ge(xnT_ready, 8 * f + pair + 1)
                    for i in (2 * pair, 2 * pair + 1):
                        for k in range(DK):
                            last = pe.matmul(bank[LBANK[pair == TPAIRS - 1]][:, i * E:(i + 1) * E], source[:, k, i * P:(i + 1) * P], wr[:, k, :],
                                             start=(k == 0), stop=(k == DK - 1))
                    if pair >= TPAIRS - 2:
                        last.then_inc(logits_done, 1)

            def route(f):
                pe.wait_ge(chosen_ready, f + 1)
                pe.wait_ge(const_step, CONSTS)
                flat = chosen[:, :, :].rearrange("p i e -> p (i e)")
                pe.matmul(bank[4][:, 0:TILES * E], before[:, :], flat, start=True, stop=False, skip_group_check=True)
                for i in range(TILES - 1):
                    left = TILES - 1 - i
                    pe.matmul(bank[4][:, (i + 1) * E:TILES * E].rearrange("p (i e) -> p i e", e=E), ones[:, :],
                              bc(chosen[:, i, :], 1, [P, left, E]), start=False, stop=(left == 1), skip_group_check=True)
                for i in range(TILES):
                    last = pe.matmul(bank[6][:, 0:E], ones[:, :], chosen[:, i, :], start=(i == 0), stop=(i == TILES - 1))
                last.then_inc(ranks_done, 1)
                warm(WARM_RANKS[f])
                pe.wait_ge(hot_ready, f + 1)
                for q in range(PAIRS):
                    last = pe.matmul(bank[7][:, 0:BLOCKS], row_hot[:, q, :], blk_pair[:, q, :], start=(q == 0),
                                     stop=(q == PAIRS - 1))
                last.then_inc(pairs_done, 1)

            def turn_block(f, j, u, gathers):
                pe.wait_ge(gathered[u], gathers * 16)
                if after_first(f, j, 1):
                    pe.wait_ge(xT_lo_ready, f * BLOCKS + j)
                for k in range(DK):
                    last = pe.transpose(bank[5][:, k * P:(k + 1) * P], xb[u][:, k * P:(k + 1) * P], ident[:, :])
                last.then_inc(xT_in_psum, 1)

            def expert(j):
                return pe.value_load(block_expert[0:1, bass.ds(j, 1)], min_val=0, max_val=E - 1)

            def project(f, j, u, half, e):
                if half == 0:
                    pe.wait_ge(xT_hi_ready, f * BLOCKS + j + 1)
                    if f == 0:
                        pe.wait_ge(w_lo_front, e + 1)
                        pe.wait_ge(w_lo_back, e + 1)
                    if after_first(f, j, 2):
                        pe.wait_ge(silu_done, f * BLOCKS + j - 1)
                elif after_first(f, j, 2):
                    pe.wait_ge(g_done, f * BLOCKS + j - 1)
                for part, (tok, wts) in enumerate(((xT_hi, w_hi), (xT_hi, w_lo), (xT_lo, w_hi))):
                    if half == 0 and part == 2:
                        pe.wait_ge(xT_lo_ready, f * BLOCKS + j + 1)
                    for k in range(DK):
                        last = pe.matmul(bank[2 * half + u][:, :], tok[u][:, k, :],
                                         wts[:, bass.ds(e, 1), k, half * H:(half + 1) * H],
                                         start=(part == 0 and k == 0), stop=(part == 2 and k == DK - 1))
                last.then_inc(b_done if half else a_done, 1)

            def turn_gated(f, j, u):
                pe.wait_ge(g_done, f * BLOCKS + j + 1)
                if after_first(f, j, 1):
                    pe.wait_ge(gT_lo_ready, f * BLOCKS + j)
                for c in range(HK):
                    last = pe.transpose(bank[4][:, c * P:(c + 1) * P], g[:, c * P:(c + 1) * P], ident[:, :])
                last.then_inc(gT_in_psum, 1)

            def combine(f, j, u):
                pe.wait_ge(gT_hi_ready, f * BLOCKS + j + 1)
                if not isinstance(j, int) or 0 < j <= SCATTERED:
                    pe.wait_ge(y_copied, f * SCATTERED + j)
                for part, (tok, wts, ready) in enumerate(((gT_hi, wo_hi[u], wo_hi_ready), (gT_hi, wo_lo, wo_lo_ready),
                                                          (gT_lo, wo_hi[u], gT_lo_ready))):
                    pe.wait_ge(ready, f * BLOCKS + j + 1)
                    for c in range(HK):
                        last = pe.matmul(bank[y_bank(j)][:, 0:D], tok[:, c, :], wts[:, c, :], start=(part == 0 and c == 0),
                                         stop=(part == 2 and c == HK - 1))
                last.then_inc(y_done, 1)

            def spread(f, j):
                k = j - SCATTERED
                pe.wait_ge(slot_hot_ready, 2 * (f * LAST + k + 1))
                pe.wait_ge(gated_lo_ready, f * LAST + k + 1)
                last_of = [k == LAST - 1 and all(pair != i for pair, _ in PE_ROWS[f]) for i in range(TPAIRS)]
                for i in range(TPAIRS):
                    for t in (2 * i, 2 * i + 1):
                        for part, rows in enumerate(gated_rows[k]):
                            last = pe.matmul(acc(t), slot_hot[k][:, t, :], rows[:, :], start=(k == 0 and part == 0 and t % 2 == 0),
                                             stop=(last_of[i] and part == 1 and t % 2 == 1), skip_group_check=True)
                    if last_of[i]:
                        last.then_inc(spread_done, 1)

            def acc(t):
                return bank[ACC_BANK[t // 2]][:, t % 2 * D:(t % 2 + 1) * D]

            def add_scaled(f):
                for n, (i, k) in enumerate(PE_ROWS[f]):
                    pe.wait_ge(y_scaled, f * len(PE_ROWS[0]) + n + 1)
                    last_of = all(pair != i for pair, _ in PE_ROWS[f][n + 1:])
                    for t in (2 * i, 2 * i + 1):
                        last = pe.matmul(acc(t), ident[:, :], y_in[:, t, k, :], start=False, stop=(last_of and t % 2 == 1),
                                         skip_group_check=True)
                    if last_of:
                        last.then_inc(spread_done, 1)

            def ffn(f):
                if f == 0:
                    for pair in range(TPAIRS):
                        turn(0, (pair,))
                        if pair == 0:
                            pe.wait_ge(router_loaded, 16)
                        else:
                            score_experts(0, (pair - 1,))
                else:
                    turn(2, (TPAIRS - 1,))
                    warm(WARM_LAST)
                score_experts(f, (TPAIRS - 1,))
                route(f)
                pe.wait_ge(plan_ready, f + 1)
                warm(WARM_PLAN[f])
                base = (EVEN * f, ODD * f)
                turn_block(f, 0, 0, base[0] + 1)
                warm(WARM_TURNED[f], 4)
                first = expert(0)
                project(f, 0, 0, 0, first)
                project(f, 0, 0, 1, first)
                second = expert(1)
                turn_block(f, 1, 1, base[1] + 1)
                project(f, 1, 1, 0, second)
                turn_gated(f, 0, 0)
                project(f, 1, 1, 1, second)

                def body(j, u, of_parity, gated_next=True, block_next=True):
                    if block_next:
                        e = expert(j + 2)
                        turn_block(f, j + 2, u, of_parity + (base[u] + 2))
                    combine(f, j, u)
                    if block_next:
                        project(f, j + 2, u, 0, e)
                    if gated_next:
                        turn_gated(f, j + 1, 1 - u)
                    if block_next:
                        project(f, j + 2, u, 1, e)

                for j in range(PEELED):
                    body(j, j % 2, j // 2)
                with pe.Fori(0, LOOPED) as i:
                    for u in range(2):
                        body(i * 2 + (PEELED + u), (PEELED + u) % 2, i + (PEELED + u) // 2)
                for j in range(AFTER, BLOCKS):
                    body(j, j % 2, j // 2, j + 1 < BLOCKS, j + 2 < BLOCKS)
                for j in range(SCATTERED, BLOCKS):
                    spread(f, j)
                add_scaled(f)

            pe.wait_ge(const_step, IDENT_CONSTS)
            warm(WARM_START)
            ffn(0)
            warm(WARM_TURN[0], 4)
            turn(1, (0,))
            warm(WARM_TURN[1], 4)
            pe.wait_ge(attn_w_loaded, 64)
            pe.wait_ge(xnT_ready, TPAIRS + 1)

            def chunk(b, c):
                if c:
                    pe.wait_ge(qk_ready, b * DK + c)
                else:
                    reach(pe, attn_added, b)
                for w, to in ((wq, 0), (wk, SEQ)):
                    for k in range(DK):
                        last = pe.matmul(bank[7][:, to:to + SEQ], w[:, k, c * P:(c + 1) * P], xnT[:, k, bass.ds(b * SEQ, SEQ)],
                                         start=(k == 0), stop=(k == DK - 1))
                last.then_inc(qk_done, 1)

            def values(first, last):
                for t in range(first, last):
                    reach(pe, v_rest_ready, t - 1 if t >= 4 else 0)
                    for k in range(DK):
                        last = pe.matmul(bank[VBANK[t]][:, 0:D], xnT[:, k, t * P:(t + 1) * P], wv[:, k, :],
                                         start=(k == 0), stop=(k == DK - 1))
                    last.then_inc(v_done, 1)

            def scores(b, s, tail):
                g = b * HPAIRS + (s - SLAG)
                c, u = (s - SLAG) % HPAIRS // CPAIRS, s % 2
                keys = k_head[s % KSLOTS]
                mask = bc(neg_mask[:, :], 1, [P, 2, P])
                if tail:
                    if (s - SLAG) % CPAIRS == 0:
                        pe.wait_ge(qk_ready, b * DK + (c + 1 - (DK if s < SLAG else 0)))
                    pe.wait_ge(k_head_ready, g + 1)
                    reach(pe, tail_probs_ready, g * 2 - 2)
                    to = bank[u][:, :].rearrange("p (h k) -> p h k", h=2)
                else:
                    reach(pe, head_probs_ready, g * 2)
                    to = bank[2][:, 0:2 * P].rearrange("p (h k) -> p h k", h=2)
                width = SEQ if tail else P
                for n, (q, part) in enumerate(((q_hi[c], 0), (q_hi[c], 1), (q_lo[c], 0))):
                    pe.matmul(to, q[:, 1 if tail else 0, :], keys[:, part, :, 0:width], start=(n == 0), stop=False)
                pe.matmul(to[:, :, width - P:width], ident_b[:, :], mask, start=False, stop=True)\
                    .then_inc(tail_scored if tail else head_scored, 1)

            def turn_probs(b, s):
                g = b * HPAIRS + (s - SLAG - 2)
                for hh in range(2):
                    pe.wait_ge(head_probs_ready, g * 2 + (hh + 1))
                    reach(pe, pT_lo_ready, g * 2 + (hh - 1))
                    for i in range(3):
                        last = pe.transpose(bank[3 + hh][:, i * P:(i + 1) * P], probs[s % 2][:, hh, i, :], ident[:, :])
                    last.then_inc(probsT_done, 1)

            def weigh(b, s):
                g = b * HPAIRS + (s - SLAG - 3)
                ago = s < SLAG + 3
                for hh in range(2):
                    h = 2 * ((s - SLAG - 3) % HPAIRS) + hh
                    u = (s - 1) % 2 * 2 + hh
                    pe.wait_ge(pT_lo_ready, g * 2 + (hh + 1))
                    both, second = slice(2 * HD * h, 2 * HD * (h + 1)), slice(2 * HD * h + HD, 2 * HD * (h + 1))
                    for i, (qt, kt) in enumerate(((0, 0), (1, 0), (1, 1))):
                        rows = v[:, bass.ds(b * 2 + (kt - 2 * ago), 1), h, :]
                        to = bank[5 + qt]
                        pe.matmul(to[:, both], pT_hi[u][:, i, :], rows[:, :, 0:2 * HD], start=(kt == 0), stop=False)
                        pe.matmul(to[:, second], pT_hi[u][:, i, :], rows[:, :, 2 * HD:3 * HD], start=False, stop=False)
                        last = pe.matmul(to[:, both], pT_lo[u][:, i, :], rows[:, :, 0:2 * HD], start=False, stop=(kt == qt))
                    last.then_inc(pv_done, 1)

            def turn_context(b, new):
                pe.wait_ge(ctx_ready, b)
                if new:
                    pe.wait_ge(qk_ready, b * DK + DK)
                for c in range(DK):
                    for qt in range(2):
                        heads = ctxv[:, qt, c * HPC:(c + 1) * HPC, :].rearrange("p h d -> p (h d)")
                        last = pe.transpose(bank[7][:, c * SEQ + qt * P:c * SEQ + (qt + 1) * P], heads, ident[:, :])
                last.then_inc(ctxT_done, 1)

            def project_out(b):
                pe.wait_ge(ctxT_ready, b)
                for qt in range(2):
                    for c in range(DK):
                        last = pe.matmul(bank[7][:, qt * D:(qt + 1) * D], ctxT[:, c, qt * P:(qt + 1) * P], wo[:, c, :],
                                         start=(c == 0), stop=(c == DK - 1))
                last.then_inc(o_done, 1)

            def step(b, old, new):
                for s in range(HPAIRS):
                    if old and s == OUT_STEP + 1:
                        project_out(b)
                        if not new:
                            turn(2, range(2, TPAIRS - 1))
                            score_experts(1, range(TPAIRS - 1))
                            warm(WARM_SCORES)
                    if old if s < SLAG else new:
                        scores(b, s, True)
                    if old if s < SLAG + 2 else new:
                        if not old and s == SLAG + 2:
                            pe.wait_ge(v_rest_ready, VALUES[SLAG][1])
                        turn_probs(b, s)
                        if not new and s >= SLAG:
                            pe.wait_ge(attn_added, BATCH)
                            warm(WARM_END, 7)
                    if not new and s == SUM_STEP:
                        turn(2, range(1))
                        warm(WARM_END, 7)
                    if old and s == OUT_STEP:
                        if not new:
                            warm(WARM_CONTEXT, 7)
                        turn_context(b, new)
                        if not new:
                            turn(2, (1,))
                    if new and s in CHUNK_STEP:
                        chunk(b, CHUNK_STEP.index(s))
                    if old if s < SLAG else new:
                        scores(b, s, False)
                    if old if s < SLAG + 3 else new:
                        if s == SLAG + 3:
                            if old:
                                pe.wait_ge(ctx_summed, b * 2)
                            else:
                                pe.wait_ge(v_rest_ready, TILES)
                                pe.wait_ge(v_ready, 2)
                        weigh(b, s)
                    if not old and s == 0:
                        turn(1, (1, 2))
                        pe.wait_ge(xnT_ready, TPAIRS + 2)
                    if not old and s == 1:
                        values(0, 1)
                        turn(1, (3,))
                        values(1, 2)
                        pe.wait_ge(xnT_ready, 2 * TPAIRS)
                    elif s in VALUES and not old:
                        values(*VALUES[s])
                if not old:
                    pe.wait_ge(v_ready, TILES)

            sweep(pe, step)
            ffn(1)


def kernel(**inputs):
    import concourse.bacc as bacc
    from concourse.bass_utils import run_bass_kernel_spmd

    def lay(name, turned=False):
        a = np.asarray(inputs[name])
        return np.ascontiguousarray(np.swapaxes(a, -1, -2) if turned else a)

    arrays = {
        "x": lay("L0_attn_inputs"),
        "wq_t": lay("L0_attn_w_q", True),
        "wk_t": lay("L0_attn_w_k", True),
        "wv_t": lay("L0_attn_w_v", True),
        "wo_t": lay("L0_attn_w_o", True),
        "bo": lay("L0_attn_b_o"),
        "wr_t": lay("L0_ffn_router_weight", True),
        "win_t": lay("L0_ffn_w_in", True),
        "wout_t": lay("L0_ffn_w_out", True),
        "bias": lay("L0_ffn_bias"),
    }
    nc = bacc.Bacc("TRN2", target_bir_lowering=False, num_devices=1)
    ins = [nc.dram_tensor(f"in_{n}", a.shape, F32, kind="ExternalInput").ap() for n, a in arrays.items()]
    out = nc.dram_tensor("out", (BATCH, SEQ, D), F32, kind="ExternalOutput").ap()
    build(nc, *ins, out)
    return run_bass_kernel_spmd(nc, [{f"in_{n}": a for n, a in arrays.items()}], core_ids=[0]).results[0]["out"]
```
